# Optimizing a Trainium2 kernel written in Bass

```python
import numpy as np
import jax
import jax.numpy as jnp

def _softmax(x, axis=-1):
    return jax.nn.softmax(x, axis=axis)

def _gelu(x):
    return jax.nn.gelu(x, approximate=True)

def _silu(x):
    return jax.nn.silu(x)

def _sigmoid(x):
    return jax.nn.sigmoid(x)

def _layernorm(x, axis=-1, eps=1e-05):
    m = jnp.mean(x, axis=axis, keepdims=True)
    v = jnp.var(x, axis=axis, keepdims=True)
    return (x - m) / jnp.sqrt(v + eps)

def _scatter_add(tgt, idx, src, axis=0):
    return tgt.at[idx].add(src)

def _segment_sum(src, seg, n):
    return jax.ops.segment_sum(src, seg, n)
kernel_name = 'mk_adj_resnorm_d1_adj_r2_a66e38'

def setup_inputs(seed: int=0):
    np.random.seed(seed)
    _w = jnp.asarray

    def _rec_inputs():
        import jax
        import jax.numpy as jnp
        _gk = jax.random.key(seed)
        x = -0.0005963 + 1.001 * jax.random.normal(jax.random.fold_in(_gk, 1), (2048, 256), jnp.float32)
        _w = (1.0 + jnp.arange(2048, dtype=jnp.float32)) ** (-0.5)
        _w = _w / _w.mean()
        _pij = jnp.clip(0.0078125 * _w[:, None] * _w[None, :], 0.0, 1.0)
        _a = jax.random.uniform(jax.random.fold_in(_gk, 2), (2048, 2048)) < _pij
        _af = _a.astype(jnp.float32)
        adj = _af
        return (x, adj)
    x, adj = _rec_inputs()

    def _L0_gnn_setup():
        import jax, jax.numpy as jnp
        import numpy as np
        N = 3072
        D_IN = 256
        D_OUT = 256
        DENSITY = 0.005
        key = jax.random.key(seed)
        ks = jax.random.split(key, 12)
        x = jax.random.normal(ks[0], (N, D_IN), dtype=jnp.float32)
        adj_a = (jax.random.uniform(ks[1], (N, N)) < DENSITY).astype(jnp.float32)
        adj_b = (jax.random.uniform(ks[2], (N, N)) < DENSITY).astype(jnp.float32)
        W_sa = jax.random.normal(ks[3], (D_IN, D_OUT), dtype=jnp.float32) * (1.414 / np.sqrt(D_IN + D_OUT))
        a_sa = jax.random.normal(ks[4], (1, 2 * D_OUT), dtype=jnp.float32) * (1.414 / np.sqrt(1 + 2 * D_OUT))
        stdv = 1.0 / np.sqrt(D_OUT)
        W_gcnb = jax.random.uniform(ks[5], (D_IN, D_OUT), minval=-stdv, maxval=stdv, dtype=jnp.float32)
        b_gcnb = jax.random.uniform(ks[6], (D_OUT,), minval=-stdv, maxval=stdv, dtype=jnp.float32)
        s = 1.0 / np.sqrt(2 * D_IN)
        Wa = jax.random.uniform(ks[7], (1, 2 * D_IN), minval=-s, maxval=s, dtype=jnp.float32)
        ba = jax.random.uniform(ks[8], (1,), minval=-s, maxval=s, dtype=jnp.float32)
        Wb = jax.random.uniform(ks[9], (1, 2 * D_IN), minval=-s, maxval=s, dtype=jnp.float32)
        bb = jax.random.uniform(ks[10], (1,), minval=-s, maxval=s, dtype=jnp.float32)
        return {'x': x, 'adj_a': adj_a, 'adj_b': adj_b, 'W_sa': W_sa, 'a_sa': a_sa, 'W_gcnb': W_gcnb, 'b_gcnb': b_gcnb, 'Wa': Wa, 'ba': ba, 'Wb': Wb, 'bb': bb}
    _L0_gnn_all = _L0_gnn_setup()
    _L0_gnn_in = {k: v for k, v in _L0_gnn_all.items() if k in ('W_sa', 'a_sa', 'W_gcnb', 'b_gcnb', 'Wa', 'ba', 'Wb', 'bb')}
    del _L0_gnn_all
    return {'x': x, 'adj': adj, 'L0_gnn_W_sa': _L0_gnn_in['W_sa'], 'L0_gnn_a_sa': _L0_gnn_in['a_sa'], 'L0_gnn_W_gcnb': _L0_gnn_in['W_gcnb'], 'L0_gnn_b_gcnb': _L0_gnn_in['b_gcnb'], 'L0_gnn_Wa': _L0_gnn_in['Wa'], 'L0_gnn_ba': _L0_gnn_in['ba'], 'L0_gnn_Wb': _L0_gnn_in['Wb'], 'L0_gnn_bb': _L0_gnn_in['bb']}

def reference(x, adj, L0_gnn_W_sa, L0_gnn_a_sa, L0_gnn_W_gcnb, L0_gnn_b_gcnb, L0_gnn_Wa, L0_gnn_ba, L0_gnn_Wb, L0_gnn_bb):
    import jax
    import jax.numpy as jnp

    def _L0_gnn_ref(x, adj_a, adj_b, W_sa, a_sa, W_gcnb, b_gcnb, Wa, ba, Wb, bb):
        import jax, jax.numpy as jnp
        import numpy as np
        N = 3072
        D_IN = 256
        D_OUT = 256
        DENSITY = 0.005
        type_sum_a = adj_a @ x
        type_sum_b = adj_b @ x
        attn_a = jax.nn.sigmoid(jnp.concatenate([type_sum_a, x], axis=1) @ Wa.T + ba)
        attn_b = jax.nn.sigmoid(jnp.concatenate([type_sum_b, x], axis=1) @ Wb.T + bb)
        h = x @ W_sa
        Hd = h.shape[1]
        s_left = h @ a_sa[0, :Hd]
        s_right = h @ a_sa[0, Hd:]
        scores = s_left[:, None] + s_right[None, :]
        e = jnp.where(adj_a != 0, jnp.exp(-jax.nn.leaky_relu(scores, 0.01)), 0.0)
        attn = e / (jnp.sum(e, axis=1, keepdims=True) + 1e-05)
        x_a = attn @ h
        x_b = adj_b @ (x @ W_gcnb) + b_gcnb
        return jax.nn.sigmoid(attn_a * x_a + attn_b * x_b)
    x = _layernorm(x + _L0_gnn_ref(x, adj, adj, L0_gnn_W_sa, L0_gnn_a_sa, L0_gnn_W_gcnb, L0_gnn_b_gcnb, L0_gnn_Wa, L0_gnn_ba, L0_gnn_Wb, L0_gnn_bb), axis=-1)
    return x

_drawn_inputs = setup_inputs


def setup_inputs(seed=0):
    import zlib

    import numpy as np

    out = dict(_drawn_inputs(seed))
    spreads = {}
    factors = {'L0_gnn_a_sa': 3.375, 'L0_gnn_b_gcnb': 8.0, 'L0_gnn_Wa': 3.152}
    for name, (base, spread) in spreads.items():
        noise = np.random.default_rng([zlib.crc32(name.encode()), seed]).standard_normal(out[name].shape)
        drawn = base * np.exp(spread * noise) if base else spread * noise
        out[name] = jnp.asarray(drawn.astype(out[name].dtype))
    for name, factor in factors.items():
        out[name] = (out[name] * factor).astype(out[name].dtype)
    return out
```

```python
import concourse.bass as bass
from concourse import mybir
from contextlib import ExitStack


def gated_two_relation_gnn_kernel(
    nc: bass.Bass,
    x: bass.AP,
    adj: bass.AP,
    W_sa: bass.AP,
    a_sa: bass.AP,
    W_g: bass.AP,
    b_g: bass.AP,
    Wa: bass.AP,
    ba: bass.AP,
    Wb: bass.AP,
    bb: bass.AP,
    out: bass.AP,
):
    fp32 = mybir.dt.float32
    f32r = mybir.dt.float32r
    u8 = mybir.dt.uint8
    ALU = mybir.AluOpType
    ACT = mybir.ActivationFunctionType
    AX = mybir.AxisListType

    P = 128
    N, D = x.shape
    NT = N // P
    NC = D // P
    PACK = 4
    NB = NT // PACK
    EW = D + 2
    MW = D + 2
    GW = D + 4
    SLOPE = 0.01
    EPS_DEN, EPS_LN = 1e-05, 1e-05

    x_v = x.rearrange("(b p q) d -> p b (q d)", b=NB, q=PACK)
    adj_v = adj.rearrange("(b p q) j -> b q p j", b=NB, q=PACK)
    out_v = out.rearrange("(b p q) d -> b q p d", b=NB, q=PACK)

    ctx = ExitStack()
    with ctx:
        def sb(name, shape, dt=fp32):
            return ctx.enter_context(nc.sbuf_tensor(name, shape, dt))

        def pb(name):
            return ctx.enter_context(nc.psum_tensor(name, [P, 512], fp32))

        def sem(name):
            return ctx.enter_context(nc.semaphore(name))

        xs = sb("xs", [P, NT, D])
        wsa = sb("wsa", [P, NC, EW])
        wg = sb("wg", [P, NC, GW])
        a_bc = sb("a_bc", [P, 2, D])
        bg_bc = sb("bg_bc", [P, D])
        gate_bias = sb("gate_bias", [P, 2])
        adj_in = sb("adj_in", [P, 2, N])
        ident = sb("ident", [P, P])
        ones = sb("ones", [P, P])
        eps = sb("eps", [P, 1])
        minus_half = sb("minus_half", [P, 1])
        x_slot = sb("x_slot", [P, 2, D])
        xT = sb("xT", [P, 2, NC, P])
        hD = sb("hD", [P, NT, EW])
        xw_hi = sb("xw_hi", [P, NT, MW], f32r)
        xw_lo = sb("xw_lo", [P, NT, MW], f32r)
        s_rl = sb("s_rl", [P, NT, 2])
        dc = sb("dc", [P, NT, 2])
        gate_own = sb("gate_own", [P, NT, 2])
        wprod = sb("wprod", [P, 2 * NC, D])
        sl_sq = sb("sl_sq", [P, 2, P])
        sl_bc = sb("sl_bc", [P, NT, P])
        mask8 = sb("mask8", [P, 2, N], u8)
        maskT = sb("maskT", [P, 2, NT, P], f32r)
        su = sb("su", [P, NT, P])
        sg = sb("sg", [P, NT, P])
        eT = sb("eT", [P, 2, NT, P])
        gz = sb("gz", [P, 2])
        gt = sb("gt", [P, 2])
        gate = sb("gate", [P, 2])
        den = sb("den", [P, 1])
        rden = sb("rden", [P, 1])
        coef = sb("coef", [P, 1])
        xb_bias = sb("xb_bias", [P, D])
        xb_gated = sb("xb_gated", [P, D])
        mix = sb("mix", [P, D])
        tmix = sb("tmix", [P, D])
        res = sb("res", [P, D])
        stats = sb("stats", [P, 6])
        mean_var = sb("mean_var", [P, 2])
        var_eps = sb("var_eps", [P, 1])
        rstd = sb("rstd", [P, 1])
        y = sb("y", [P, 2, D])

        pT = [pb("pT0"), pb("pT1")]
        pE = [pb("pE0"), pb("pE1")]
        pM = [pb("pM0"), pb("pM1")]
        pS = [pb("pS0"), pb("pS1")]

        x_in = [sem(f"x_in{b}") for b in range(NB)]
        w_in = sem("w_in")
        small_in = sem("small_in")
        adj_arrived = [sem("adj_arrived0"), sem("adj_arrived1")]
        zeros_set = sem("zeros_set")
        const = sem("const")
        wprod_done = sem("wprod_done")
        wcol_done = sem("wcol_done")
        x_slot_full = sem("x_slot_full")
        xT_made = sem("xT_made")
        xT_copied = sem("xT_copied")
        proj_done = sem("proj_done")
        dc_done = sem("dc_done")
        hi_done = sem("hi_done")
        sq_done = sem("sq_done")
        pE_read = sem("pE_read")
        pM_read = sem("pM_read")
        hD_col_done = sem("hD_col_done")
        slT_made = sem("slT_made")
        sl_bc_done = sem("sl_bc_done")
        encoded = sem("encoded")
        maskT_made = sem("maskT_made")
        decoded = sem("decoded")
        su_done = sem("su_done")
        sg_done = sem("sg_done")
        eT_done = sem("eT_done")
        sums_done = sem("sums_done")
        gz_done = sem("gz_done")
        gt_done = sem("gt_done")
        gate_done = sem("gate_done")
        den_done = sem("den_done")
        rden_done = sem("rden_done")
        coef_done = sem("coef_done")
        xb_bias_done = sem("xb_bias_done")
        xb_gated_done = sem("xb_gated_done")
        mix_done = sem("mix_done")
        tmix_done = sem("tmix_done")
        res_done = sem("res_done")
        stats_done = sem("stats_done")
        var_done = sem("var_done")
        var_eps_done = sem("var_eps_done")
        rstd_done = sem("rstd_done")
        y_done = sem("y_done")
        y_out = [sem("y_out0"), sem("y_out1")]

        block = ctx.enter_context(nc.Block())

        def steps(eng, first, last, body):
            pairs = (last - first) // 2
            if pairs > 1:
                with eng.Fori(0, pairs) as r:
                    for t in (first, first + 1):
                        body(r * 2 + t, t % 2, r + t // 2)
            else:
                for t in range(first, first + 2 * pairs):
                    body(t, t % 2, t // 2)
            if (last - first) % 2:
                body(last - 1, (last - 1) % 2, (last - 1) // 2)

        def from_tile(t, n):
            return not isinstance(t, int) or t >= n

        @block.sync
        def _(sp):
            for b in range(NB):
                sp.dma_start(xs[:, PACK * b:PACK * (b + 1), :].rearrange("p q d -> p (q d)"),
                             x_v[:, b, :]).then_inc(x_in[b], 16)

            def load(b, q):
                sp.dma_start(adj_in[:, q % 2, :], adj_v[b, q]).then_inc(adj_arrived[q % 2], 16)

            def store(b, q):
                sp.wait_ge(y_done, b * PACK + (q + 1))
                sp.dma_start(out_v[b, q], y[:, q % 2, :]).then_inc(y_out[q % 2], 16)

            load(0, 0)
            load(0, 1)
            for q in range(2, PACK):
                sp.wait_ge(encoded, q - 1)
                load(0, q)
            with sp.Fori(0, NB - 1) as b:
                for q in range(PACK):
                    sp.wait_ge(encoded, b * PACK + (q + PACK - 1))
                    load(b + 1, q)
                    store(b, q)
            for q in range(PACK):
                store(NB - 1, q)
            for slot in range(2):
                sp.wait_ge(y_out[slot], 16 * (NT // 2))

        @block.gpsimd
        def _(pool):
            nc.gpsimd.memset(ident[:], 0.0).then_inc(zeros_set, 1)
            pool.wait_ge(zeros_set, 1)
            nc.gpsimd.affine_select(out=ident[:], in_=ident[:], compare_op=ALU.not_equal, fill=1.0,
                                    base=0, pattern=[[-1, P]], channel_multiplier=1).then_inc(const, 1)
            nc.gpsimd.memset(ones[:], 1.0).then_inc(const, 1)
            nc.gpsimd.memset(eps[:], EPS_LN).then_inc(const, 1)
            nc.gpsimd.memset(minus_half[:], -0.5).then_inc(const, 1)
            nc.gpsimd.memset(hD[:, :, D + 1], 0.0).then_inc(const, 1)

            def fill_slot(k, slot, _):
                if from_tile(k, 2):
                    pool.wait_ge(xT_made, k - 1)
                nc.gpsimd.tensor_copy(x_slot[:, slot, :], xs[:, k, :]).then_inc(x_slot_full, 1)

            for b in range(NB):
                pool.wait_ge(x_in[b], 16)
                if b == 0:
                    fill_slot(0, 0, 0)
                    fill_slot(1, 1, 0)
                    steps(pool, 2, PACK, fill_slot)
                else:
                    steps(pool, PACK * b, PACK * (b + 1), fill_slot)

            def inverse_deviation(t, *_):
                pool.wait_ge(var_done, t + 1)
                nc.gpsimd.tensor_tensor(var_eps[:], mean_var[:, 1:2], eps[:], ALU.add).then_inc(var_eps_done, 1)
                pool.wait_ge(var_eps_done, t + 1)
                nc.gpsimd.tensor_tensor(rstd[:], var_eps[:], minus_half[:], ALU.pow).then_inc(rstd_done, 1)

            pool.wait_ge(const, 5)
            steps(pool, 0, NT, inverse_deviation)

        @block.scalar
        def _(act):
            act.dma_start(wsa[:, :, 0:D], W_sa.rearrange("(c p) n -> p c n", p=P)).then_inc(w_in, 16)
            act.dma_start(a_bc[:].rearrange("p s n -> p (s n)"), a_sa.to_broadcast([P, 2 * D])).then_inc(w_in, 16)
            act.dma_start(wg[:, :, 0:D], W_g.rearrange("(c p) n -> p c n", p=P)).then_inc(w_in, 16)
            with nc.allow_non_contiguous_dma(reason="columns of 128 weights"):
                for n, w in enumerate((Wa, Wb)):
                    for half in range(2):
                        col = D + 2 * half + n
                        act.dma_start(wg[:, :, col], w[0, half * D:(half + 1) * D].rearrange("(c p) -> p c", p=P)
                                      ).then_inc(w_in, 16)
            act.dma_start(bg_bc[:], b_g.rearrange("(o n) -> o n", o=1).to_broadcast([P, D])).then_inc(small_in, 16)
            act.dma_start(gate_bias[:, 0:1], ba.rearrange("(o n) -> o n", o=1).to_broadcast([P, 1])).then_inc(small_in, 16)
            act.dma_start(gate_bias[:, 1:2], bb.rearrange("(o n) -> o n", o=1).to_broadcast([P, 1])).then_inc(small_in, 16)

            def projected(k, slot, _):
                act.wait_ge(proj_done, k + 1)
                nc.scalar.activation(dc[:, k, :], pE[slot][:, D:D + 2], ACT.Exp, scale=-SLOPE).then_inc(dc_done, 1)
                nc.scalar.activation(xw_hi[:, k, :], pM[slot][:, 0:MW], ACT.Copy).then_inc(hi_done, 1)

            def keep_sl(k, slot, _):
                act.wait_ge(slT_made, k + 1)
                nc.scalar.activation(sl_bc[:, k, :], pS[slot][:, 0:P], ACT.Copy).then_inc(sl_bc_done, 1)

            def projected_and_keep(k, slot, half):
                projected(k, slot, half)
                keep_sl(k - 1, 1 - slot, half)

            projected(0, 0, 0)
            steps(act, 1, NT, projected_and_keep)
            keep_sl(NT - 1, 1, 0)

            def decode(t, slot):
                act.wait_ge(maskT_made, t + 1)
                if from_tile(t, 2):
                    act.wait_ge(sums_done, t - 1)
                nc.scalar.activation(
                    maskT[:, slot].rearrange("p (b q) i -> p b q i", q=PACK),
                    pT[slot][:, :].bitcast(u8).rearrange("p (b i q) -> p b q i", b=NB, q=PACK),
                    ACT.Copy, bias=-1.0).then_inc(decoded, 1)

            def exponentials(t):
                act.wait_ge(su_done, t + 1)
                if from_tile(t, 1):
                    act.wait_ge(eT_done, t)
                nc.scalar.activation(sg[:].rearrange("p k i -> p (k i)"), su[:].rearrange("p k i -> p (k i)"),
                                     ACT.Exp, scale=SLOPE - 1.0).then_inc(sg_done, 1)

            def gates(t):
                act.wait_ge(gz_done, t + 1)
                nc.scalar.activation(gt[:], gz[:], ACT.Tanh, scale=0.5).then_inc(gt_done, 1)

            def squash(t):
                act.wait_ge(mix_done, t + 1)
                nc.scalar.activation(tmix[:], mix[:], ACT.Tanh, scale=0.5).then_inc(tmix_done, 1)

            decode(0, 0)
            exponentials(0)
            decode(1, 1)
            exponentials(1)

            def beside_sums(t, slot, _):
                decode(t + 1, 1 - slot)
                gates(t - 1)
                exponentials(t + 1)
                squash(t - 1)

            steps(act, 1, NT - 1, beside_sums)
            for t in (NT - 2, NT - 1):
                gates(t)
                squash(t)

        @block.vector
        def _(dve):
            dve.wait_ge(w_in, 16 * 7)
            n = 0
            for c in range(NC):
                for side, col in ((1, D), (0, D + 1)):
                    nc.vector.tensor_tensor(wprod[:, n, :], wsa[:, c, 0:D], a_bc[:, side, :], ALU.mult).then_inc(wprod_done, 1)
                    n += 1
                    dve.wait_ge(wprod_done, n)
                    nc.vector.reduce_sum(wsa[:, c, col:col + 1], wprod[:, n - 1, :], axis=AX.X).then_inc(wcol_done, 1)

            def copy_xT(k, slot):
                dve.wait_ge(xT_made, k + 1)
                if from_tile(k, 2):
                    dve.wait_ge(proj_done, k - 1)
                nc.vector.tensor_copy(xT[:, slot].rearrange("p c i -> p (c i)"), pT[slot][:, 0:D]).then_inc(xT_copied, 1)

            def projected(k, slot):
                dve.wait_ge(dc_done, k + 1)
                if from_tile(k, 2):
                    dve.wait_ge(slT_made, k - 1)
                nc.vector.tensor_scalar(sl_sq[:, slot, :], ones[:], pE[slot][:, D + 1:D + 2], None,
                                        ALU.mult).then_inc(sq_done, 1)
                nc.vector.tensor_scalar(hD[:, k, 0:D], pE[slot][:, 0:D], dc[:, k, 0:1], None, ALU.mult)
                nc.vector.tensor_copy(s_rl[:, k, :], pE[slot][:, D:D + 2]).then_inc(pE_read, 1)
                dve.wait_ge(hi_done, k + 1)
                nc.vector.tensor_tensor(xw_lo[:, k, :], pM[slot][:, 0:MW], xw_hi[:, k, :].bitcast(fp32), ALU.subtract)
                nc.vector.tensor_tensor(gate_own[:, k, :], pM[slot][:, MW:GW], gate_bias[:], ALU.add).then_inc(pM_read, 1)

            def copy_and_projected(k, slot, _):
                copy_xT(k + 1, 1 - slot)
                projected(k, slot)

            def encode(t, slot, half):
                dve.wait_ge(adj_arrived[slot], half * 16 + 16)
                if from_tile(t, 2):
                    dve.wait_ge(maskT_made, t - 1)
                nc.vector.tensor_scalar(mask8[:, slot, :], adj_in[:, slot, :], 0.0, 1.0,
                                        ALU.not_equal, ALU.add).then_inc(encoded, 1)

            dve.wait_ge(const, 5)
            dve.wait_ge(small_in, 48)
            copy_xT(0, 0)
            copy_and_projected(0, 0, 0)
            copy_and_projected(1, 1, 0)
            steps(dve, 2, NT // 2, copy_and_projected)
            encode(0, 0, 0)
            steps(dve, NT // 2, NT - 1, copy_and_projected)
            encode(1, 1, 0)
            projected(NT - 1, 1)
            nc.vector.tensor_copy(hD[:, :, D], dc[:, :, 0]).then_inc(hD_col_done, 1)
            dve.wait_ge(pE_read, NT)
            dve.wait_ge(pM_read, NT)
            dve.wait_ge(sl_bc_done, NT)

            def add_s(t):
                if from_tile(t, 1):
                    dve.wait_ge(sg_done, t)
                nc.vector.tensor_tensor(su[:], sl_bc[:, t, :].unsqueeze(1).to_broadcast([P, NT, P]),
                                        s_rl[:, :, 0].unsqueeze(2).to_broadcast([P, NT, P]), ALU.add).then_inc(su_done, 1)

            def weigh(t, slot):
                dve.wait_ge(sg_done, t + 1)
                dve.wait_ge(decoded, t + 1)
                if from_tile(t, 2):
                    dve.wait_ge(sums_done, t - 1)
                flat = "p k i -> p (k i)"
                nc.vector.scalar_tensor_tensor(eT[:, slot].rearrange(flat), sg[:].rearrange(flat), 1.0,
                                               maskT[:, slot].bitcast(fp32).rearrange(flat),
                                               ALU.min, ALU.mult).then_inc(eT_done, 1)

            def gate_logits(t, slot):
                dve.wait_ge(sums_done, t + 1)
                nc.vector.tensor_tensor(gz[:], pM[slot][:, D:D + 2], gate_own[:, t, :], ALU.add).then_inc(gz_done, 1)
                nc.vector.tensor_scalar(den[:], pE[slot][:, D:D + 1], dc[:, t, 1:2], EPS_DEN,
                                        ALU.mult, ALU.add).then_inc(den_done, 1)
                dve.wait_ge(den_done, t + 1)
                nc.vector.reciprocal(rden[:], den[:]).then_inc(rden_done, 1)

            def mix_sums(t, slot):
                dve.wait_ge(gt_done, t + 1)
                nc.vector.tensor_scalar(gate[:], gt[:], 0.5, 0.5, ALU.mult, ALU.add).then_inc(gate_done, 1)
                dve.wait_ge(gate_done, t + 1)
                dve.wait_ge(rden_done, t + 1)
                nc.vector.tensor_scalar(coef[:], gate[:, 0:1], dc[:, t, 1:2], rden[:, 0:1],
                                        ALU.mult, ALU.mult).then_inc(coef_done, 1)
                nc.vector.tensor_scalar(xb_bias[:], bg_bc[:], gate[:, 1:2], None, ALU.mult).then_inc(xb_bias_done, 1)
                dve.wait_ge(xb_bias_done, t + 1)
                nc.vector.scalar_tensor_tensor(xb_gated[:], pM[slot][:, 0:D], gate[:, 1:2], xb_bias[:],
                                               ALU.mult, ALU.add).then_inc(xb_gated_done, 1)
                dve.wait_ge(coef_done, t + 1)
                dve.wait_ge(xb_gated_done, t + 1)
                nc.vector.scalar_tensor_tensor(mix[:], pE[slot][:, 0:D], coef[:, 0:1], xb_gated[:],
                                               ALU.mult, ALU.add).then_inc(mix_done, 1)

            def residual(t):
                dve.wait_ge(tmix_done, t + 1)
                nc.vector.scalar_tensor_tensor(res[:], tmix[:], 0.5, xs[:, t, :], ALU.mult, ALU.add).then_inc(res_done, 1)
                dve.wait_ge(res_done, t + 1)
                nc.vector.bn_stats(stats[:], res[:]).then_inc(stats_done, 1)

            def variance(t):
                nc.vector.bn_aggr(mean_var[:], stats[:]).then_inc(var_done, 1)

            def normalise(t, slot, half):
                dve.wait_ge(rstd_done, t + 1)
                if from_tile(t, 2):
                    dve.wait_ge(y_out[slot], half * 16)
                nc.vector.tensor_scalar(y[:, slot, :], res[:], mean_var[:, 0:1], rstd[:, 0:1],
                                        ALU.subtract, ALU.mult).then_inc(y_done, 1)

            add_s(0)
            weigh(0, 0)
            add_s(1)
            encode(2, 0, 1)
            weigh(1, 1)

            def beside_sums(t, slot, half):
                add_s(t + 1)
                if from_tile(t, 2):
                    normalise(t - 2, slot, half - 1)
                gate_logits(t - 1, 1 - slot)
                mix_sums(t - 1, 1 - slot)
                if not isinstance(t, int) or t + 2 < NT:
                    encode(t + 2, slot, half + 1)
                residual(t - 1)
                dve.wait_ge(stats_done, t)
                weigh(t + 1, 1 - slot)
                variance(t - 1)

            for t in (1, 2, 3):
                beside_sums(t, t % 2, t // 2)
            steps(dve, 4, NT - 2, beside_sums)
            beside_sums(NT - 2, 0, NT // 2 - 1)
            normalise(NT - 3, 1, NT // 2 - 2)
            for t in (NT - 2, NT - 1):
                gate_logits(t, t % 2)
                mix_sums(t, t % 2)
                residual(t)
                dve.wait_ge(stats_done, t + 1)
                variance(t)
                normalise(t, t % 2, t // 2)

        @block.tensor
        def _(pe):
            def transpose_x(k, slot):
                pe.wait_ge(x_slot_full, k + 1)
                if from_tile(k, 2):
                    pe.wait_ge(xT_copied, k - 1)
                for c in range(NC):
                    last = nc.tensor.transpose(pT[slot][:, c * P:(c + 1) * P], x_slot[:, slot, c * P:(c + 1) * P], ident[:])
                last.then_inc(xT_made, 1)

            def project(k, slot):
                pe.wait_ge(xT_copied, k + 1)
                if from_tile(k, 2):
                    pe.wait_ge(pE_read, k - 1)
                    pe.wait_ge(pM_read, k - 1)
                for c in range(NC):
                    nc.tensor.matmul(pE[slot][:, 0:EW], xT[:, slot, c, :], wsa[:, c, :], start=c == 0, stop=c == NC - 1)
                for c in range(NC):
                    last = nc.tensor.matmul(pM[slot][:, 0:GW], xT[:, slot, c, :], wg[:, c, :],
                                            start=c == 0, stop=c == NC - 1)
                last.then_inc(proj_done, 1)

            def transpose_sl(k, slot):
                pe.wait_ge(sq_done, k + 1)
                if from_tile(k, 2):
                    pe.wait_ge(sl_bc_done, k - 1)
                nc.tensor.transpose(pS[slot][:, 0:P], sl_sq[:, slot, :], ident[:]).then_inc(slT_made, 1)

            def all_three(k, slot, _):
                transpose_x(k + 1, 1 - slot)
                project(k, slot)
                transpose_sl(k - 1, 1 - slot)

            pe.wait_ge(const, 5)
            transpose_x(0, 0)
            transpose_x(1, 1)
            pe.wait_ge(w_in, 16 * 7)
            pe.wait_ge(wcol_done, 2 * NC)
            project(0, 0)
            all_three(1, 1, 0)
            all_three(2, 0, 1)
            steps(pe, 3, NT - 1, all_three)
            project(NT - 1, 1)
            transpose_sl(NT - 2, 0)
            transpose_sl(NT - 1, 1)

            def transpose_mask(t, slot):
                pe.wait_ge(encoded, t + 1)
                if from_tile(t, 2):
                    pe.wait_ge(decoded, t - 1)
                words = mask8[:, slot, :].bitcast(fp32)
                for b in range(NB):
                    last = nc.tensor.transpose(pT[slot][:, b * P:(b + 1) * P], words[:, b * P:(b + 1) * P], ident[:])
                last.then_inc(maskT_made, 1)

            def sums(t, slot):
                pe.wait_ge(decoded, t + 1)
                pe.wait_ge(eT_done, t + 1)
                if from_tile(t, 2):
                    pe.wait_ge(mix_done, t - 1)
                for k in range(NT):
                    ends = dict(start=k == 0, stop=k == NT - 1)
                    nc.tensor.matmul(pE[slot][:, 0:EW], eT[:, slot, k, :], hD[:, k, :], **ends)
                    nc.tensor.matmul(pM[slot][:, 0:MW], maskT[:, slot, k, :], xw_hi[:, k, :], start=k == 0, stop=False)
                    last = nc.tensor.matmul(pM[slot][:, 0:MW], maskT[:, slot, k, :], xw_lo[:, k, :],
                                            start=False, stop=k == NT - 1)
                last.then_inc(sums_done, 1)

            pe.wait_ge(xT_copied, NT)
            transpose_mask(0, 0)
            transpose_mask(1, 1)
            pe.wait_ge(hD_col_done, 1)
            pe.wait_ge(hi_done, NT)
            pe.wait_ge(pM_read, NT)
            sums(0, 0)

            def transposes_and_sums(t, slot, _):
                transpose_mask(t + 1, 1 - slot)
                sums(t, slot)

            transposes_and_sums(1, 1, 0)
            steps(pe, 2, NT - 1, transposes_and_sums)
            sums(NT - 1, 1)


_INS = ['x', 'adj', 'L0_gnn_W_sa', 'L0_gnn_a_sa', 'L0_gnn_W_gcnb', 'L0_gnn_b_gcnb', 'L0_gnn_Wa', 'L0_gnn_ba',
        'L0_gnn_Wb', 'L0_gnn_bb']
_OUT_SHAPE, _OUT_DTYPE = (2048, 256), 'float32'


def kernel(**inputs):
    import numpy as _np
    import concourse.bacc as _bacc
    from concourse import mybir as _mybir
    from concourse.bass_utils import run_bass_kernel_spmd as _run

    nc = _bacc.Bacc("TRN2", target_bir_lowering=False, num_devices=1)
    arrays, args = {}, []
    for name in _INS:
        a = _np.ascontiguousarray(inputs[name])
        arrays[f"in_{name}_dram"] = a
        args.append(nc.dram_tensor(f"in_{name}_dram", a.shape, _mybir.dt.from_np(a.dtype), kind="ExternalInput").ap())
    args.append(nc.dram_tensor("out_dram", _OUT_SHAPE, _mybir.dt.from_np(_np.dtype(_OUT_DTYPE)),
                               kind="ExternalOutput").ap())
    gated_two_relation_gnn_kernel(nc, *args)
    r = _run(nc, [arrays], core_ids=[0])
    return r.results[0]["out_dram"]
```

```python
import concourse.bass as bass
from concourse import mybir
from contextlib import ExitStack


def gated_two_relation_gnn_kernel(
    nc: bass.Bass,
    x: bass.AP,
    adj: bass.AP,
    W_sa: bass.AP,
    a_sa: bass.AP,
    W_g: bass.AP,
    b_g: bass.AP,
    Wa: bass.AP,
    ba: bass.AP,
    Wb: bass.AP,
    bb: bass.AP,
    out: bass.AP,
):
    fp32 = mybir.dt.float32
    f32r = mybir.dt.float32r
    u32 = mybir.dt.uint32
    ALU = mybir.AluOpType
    ACT = mybir.ActivationFunctionType
    AX = mybir.AxisListType

    P = 128
    N, D = x.shape
    NT = N // P
    NC = D // P
    S = 32
    B = P // S
    NG = 4
    G = NT // NG
    EW = D + 1
    MW = D + 2
    HW = D + 4
    SLOPE = 0.01
    EPS_DEN, EPS_LN = 1e-05, 1e-05

    x_v = x.rearrange("(b k s) d -> b s k d", b=B, s=S)
    adj_v = adj.rearrange("(b t s) (a n) -> b t a s n", b=B, s=S, a=B)
    out_v = out.rearrange("(b t s) d -> t b s d", b=B, s=S)

    ctx = ExitStack()
    with ctx:
        def sb(name, shape, dt=fp32):
            return ctx.enter_context(nc.sbuf_tensor(name, shape, dt))

        def pb(name):
            return ctx.enter_context(nc.psum_tensor(name, [P, 512], fp32))

        def sem(name):
            return ctx.enter_context(nc.semaphore(name))

        xs = sb("xs", [P, NT, D])
        wsa = sb("wsa", [P, NC, HW])
        wg = sb("wg", [P, NC, MW])
        gate_rows = sb("gate_rows", [4, D])
        a_bc = sb("a_bc", [P, 2, D])
        bg_bc = sb("bg_bc", [P, D])
        gate_bias = sb("gate_bias", [P, 2])
        adj_in = sb("adj_in", [P, 2, B, N // B])
        ident = sb("ident", [P, P])
        ones = sb("ones", [P, P])
        eps = sb("eps", [P, 1])
        minus_half = sb("minus_half", [P, 1])
        x_slot = sb("x_slot", [P, 2, D])
        xT = sb("xT", [P, 2, NC, P])
        hD = sb("hD", [P, NT, EW + 1])
        xw_hi = sb("xw_hi", [P, NT, MW], f32r)
        xw_lo = sb("xw_lo", [P, NT, MW], f32r)
        s_own = sb("s_own", [P, NT, 4])
        gate_own = sb("gate_own", [P, NT, 2])
        wprod = sb("wprod", [P, 2 * NC, D])
        sl_sq = sb("sl_sq", [P, 2, P])
        sl_bc = sb("sl_bc", [P, NT, P])
        adjT = sb("adjT", [P, 2, NT, P])
        maskT = sb("maskT", [P, 2, NT, P], f32r)
        sg = sb("sg", [P, NT, P])
        eT = sb("eT", [P, 2, NT, P])
        gz = sb("gz", [P, 2])
        gt = sb("gt", [P, 2])
        gate = sb("gate", [P, 2])
        den = sb("den", [P, 1])
        rden = sb("rden", [P, 1])
        coef = sb("coef", [P, 1])
        xb_bias = sb("xb_bias", [P, D])
        xb_gated = sb("xb_gated", [P, D])
        mix = sb("mix", [P, D])
        tmix = sb("tmix", [P, D])
        res = sb("res", [P, D])
        stats = sb("stats", [P, 6])
        mean_var = sb("mean_var", [P, 2])
        var_eps = sb("var_eps", [P, 1])
        rstd = sb("rstd", [P, 1])
        y = sb("y", [P, 2, D])

        pT = [pb("pT0"), pb("pT1")]
        pE = [pb("pE0"), pb("pE1")]
        pM = [pb("pM0"), pb("pM1")]
        pS = pb("pS")
        pU = pb("pU")

        x_in = [sem(f"x_in{g}") for g in range(NG)]
        rows_in = sem("rows_in")
        wsa_in = sem("wsa_in")
        wg_in = sem("wg_in")
        small_in = sem("small_in")
        adj_arrived = [sem("adj_arrived0"), sem("adj_arrived1")]
        zeros_set = sem("zeros_set")
        const = sem("const")
        wprod_done = sem("wprod_done")
        wcol_done = sem("wcol_done")
        x_slot_full = sem("x_slot_full")
        xT_made = sem("xT_made")
        xT_copied = sem("xT_copied")
        proj_m_done = sem("proj_m_done")
        proj_done = sem("proj_done")
        gate_cols_made = sem("gate_cols_made")
        gate_cols_copied = sem("gate_cols_copied")
        dc_done = sem("dc_done")
        gate_own_done = sem("gate_own_done")
        hi_done = sem("hi_done")
        s_own_done = sem("s_own_done")
        sq_done = sem("sq_done")
        pE_read = sem("pE_read")
        pM_read = sem("pM_read")
        slT_made = sem("slT_made")
        sl_bc_done = sem("sl_bc_done")
        adjT_done = sem("adjT_done")
        maskT_done = sem("maskT_done")
        sg_done = sem("sg_done")
        sg0_done = sem("sg0_done")
        eT0_done = sem("eT0_done")
        eT_done = sem("eT_done")
        nbr_done = sem("nbr_done")
        att_done = sem("att_done")
        gz_done = sem("gz_done")
        gt_done = sem("gt_done")
        gate_done = sem("gate_done")
        den_done = sem("den_done")
        rden_done = sem("rden_done")
        coef_done = sem("coef_done")
        xb_bias_done = sem("xb_bias_done")
        xb_gated_done = sem("xb_gated_done")
        mix_done = sem("mix_done")
        tmix_done = sem("tmix_done")
        res_done = sem("res_done")
        stats_done = sem("stats_done")
        var_done = sem("var_done")
        var_eps_done = sem("var_eps_done")
        rstd_done = sem("rstd_done")
        y_done = sem("y_done")
        y_out = [sem("y_out0"), sem("y_out1")]

        block = ctx.enter_context(nc.Block())

        def steps(eng, first, last, body):
            pairs = (last - first) // 2
            if pairs > 1:
                with eng.Fori(0, pairs) as r:
                    for t in (first, first + 1):
                        body(r * 2 + t, t % 2, r + t // 2)
            else:
                for t in range(first, first + 2 * pairs):
                    body(t, t % 2, t // 2)
            if (last - first) % 2:
                body(last - 1, (last - 1) % 2, (last - 1) // 2)

        def from_tile(t, n):
            return not isinstance(t, int) or t >= n

        @block.sync
        def _(sp):
            def load_x(g):
                for b in range(B):
                    sp.dma_start(xs[S * b:S * (b + 1), G * g:G * (g + 1), :],
                                 x_v[b, :, G * g:G * (g + 1), :]).then_inc(x_in[g], 16)

            def load(t, slot):
                for b in range(B):
                    sp.dma_start(adj_in[:, slot, b, :],
                                 adj_v[b, t]).then_inc(adj_arrived[slot], 16)

            def store(t, slot):
                sp.wait_ge(y_done, t + 1)
                sp.dma_start(out_v[t], y[:, slot, :]).then_inc(y_out[slot], 16)

            def load_ahead(t, slot, _):
                sp.wait_ge(adjT_done, t + 1)
                load(t + 2, slot)
                if from_tile(t, 2):
                    store(t - 2, slot)

            load_x(0)
            sp.dma_start(wg[:, :, 0:D], W_g.rearrange("(c p) n -> p c n", p=P)).then_inc(wg_in, 16)
            sp.wait_ge(x_in[0], 16 * B)
            for g in range(1, NG):
                load_x(g)
            load(0, 0)
            load(1, 1)
            load_ahead(0, 0, 0)
            load_ahead(1, 1, 0)
            steps(sp, 2, NT - 2, load_ahead)
            for t in range(NT - 4, NT):
                store(t, t % 2)
            for slot in range(2):
                sp.wait_ge(y_out[slot], 16 * (NT // 2))

        @block.gpsimd
        def _(pool):
            nc.gpsimd.memset(ident[:], 0.0).then_inc(zeros_set, 1)
            pool.wait_ge(zeros_set, 1)
            nc.gpsimd.affine_select(out=ident[:], in_=ident[:], compare_op=ALU.not_equal, fill=1.0,
                                    base=0, pattern=[[-1, P]], channel_multiplier=1).then_inc(const, 1)
            nc.gpsimd.memset(ones[:], 1.0).then_inc(const, 1)
            nc.gpsimd.memset(eps[:], EPS_LN).then_inc(const, 1)
            nc.gpsimd.memset(minus_half[:], -0.5).then_inc(const, 1)

            def fill_slot(k, slot):
                if from_tile(k, 4):
                    pool.wait_ge(xT_made, k - 1)
                nc.gpsimd.tensor_copy(x_slot[:, slot, :], xs[:, k, :]).then_inc(x_slot_full, 1)

            def repeat_sl(k, slot):
                pool.wait_ge(s_own_done, k + 1)
                if from_tile(k, 2):
                    pool.wait_ge(slT_made, k - 1)
                nc.gpsimd.tensor_tensor(sl_sq[:, slot, :], ones[:], s_own[:, k, 1:2].to_broadcast([P, P]),
                                        ALU.mult).then_inc(sq_done, 1)

            def fill_and_repeat(k, slot, _):
                fill_slot(k, slot)
                repeat_sl(k - 2, slot)

            pool.wait_ge(const, 4)
            pool.wait_ge(x_in[0], 16 * B)
            fill_slot(2, 0)
            fill_slot(3, 1)
            repeat_sl(0, 0)
            repeat_sl(1, 1)
            for g in range(1, NG):
                pool.wait_ge(x_in[g], 16 * B)
                steps(pool, G * g, G * (g + 1), fill_and_repeat)
            for k in (NT - 2, NT - 1):
                repeat_sl(k, k % 2)

            def inverse_deviation(t, *_):
                pool.wait_ge(var_done, t + 1)
                nc.gpsimd.tensor_tensor(var_eps[:], mean_var[:, 1:2], eps[:], ALU.add).then_inc(var_eps_done, 1)
                pool.wait_ge(var_eps_done, t + 1)
                nc.gpsimd.tensor_tensor(rstd[:], var_eps[:], minus_half[:], ALU.pow).then_inc(rstd_done, 1)

            steps(pool, 0, NT, inverse_deviation)

        @block.scalar
        def _(act):
            act.dma_start(wsa[:, :, 0:D], W_sa.rearrange("(c p) n -> p c n", p=P)).then_inc(wsa_in, 16)
            for n, w in enumerate((Wa, Wb)):
                act.dma_start(gate_rows[n:n + 3:2, :], w.rearrange("o (s n) -> (o s) n", s=2)).then_inc(rows_in, 16)
            act.dma_start(a_bc[:].rearrange("p s n -> p (s n)"), a_sa.to_broadcast([P, 2 * D])).then_inc(wsa_in, 16)
            act.dma_start(bg_bc[:], b_g.rearrange("(o n) -> o n", o=1).to_broadcast([P, D])).then_inc(small_in, 16)
            act.dma_start(gate_bias[:, 0:1], ba.rearrange("(o n) -> o n", o=1).to_broadcast([P, 1])).then_inc(small_in, 16)
            act.dma_start(gate_bias[:, 1:2], bb.rearrange("(o n) -> o n", o=1).to_broadcast([P, 1])).then_inc(small_in, 16)

            act.wait_ge(gate_cols_made, 1)
            cols = pU[:, 0:4 * NC].rearrange("p (c n) -> p c n", c=NC)
            nc.scalar.activation(wg[:, :, D:D + 2], cols[:, :, 0:2], ACT.Copy).then_inc(gate_cols_copied, 1)
            nc.scalar.activation(wsa[:, :, D + 2:D + 4], cols[:, :, 2:4], ACT.Copy).then_inc(gate_cols_copied, 1)

            def projected(k, slot):
                act.wait_ge(proj_m_done, k + 1)
                nc.scalar.activation(xw_hi[:, k, :], pM[slot][:, 0:MW], ACT.Copy).then_inc(hi_done, 1)
                act.wait_ge(proj_done, k + 1)
                nc.scalar.activation(hD[:, k, D:D + 2], pE[slot][:, D:D + 2], ACT.Exp,
                                     scale=SLOPE / (1.0 - SLOPE)).then_inc(dc_done, 1)

            def keep_sl(k):
                act.wait_ge(slT_made, k + 1)
                nc.scalar.activation(sl_bc[:, k, :], pS[:, 0:P], ACT.Copy).then_inc(sl_bc_done, 1)

            def exponentials_0(k):
                act.wait_ge(s_own_done, k + 1)
                nc.scalar.activation(sg[:, k, :], sl_bc[:, 0, :], ACT.Exp, bias=s_own[:, k, 0:1]).then_inc(sg0_done, 1)

            def projected_and_last(k, slot, _):
                projected(k, slot)
                keep_sl(k - 1)
                exponentials_0(k - 1)

            def round_mask(t, slot):
                act.wait_ge(adjT_done, t + 1)
                if from_tile(t, 2):
                    act.wait_ge(att_done, t - 1)
                nc.scalar.activation(maskT[:, slot].rearrange("p k i -> p (k i)"),
                                     adjT[:, slot].rearrange("p k i -> p (k i)"), ACT.Copy).then_inc(maskT_done, 1)

            def exponentials(t):
                if from_tile(t, 2):
                    act.wait_ge(eT_done, t - 1)
                else:
                    act.wait_ge(eT0_done, NG)
                for k in range(NT):
                    last = nc.scalar.activation(sg[:, k, :], sl_bc[:, t, :], ACT.Exp, bias=s_own[:, k, 0:1])
                last.then_inc(sg_done, 1)

            def gates(t):
                act.wait_ge(gz_done, t + 1)
                nc.scalar.activation(gt[:], gz[:], ACT.Tanh, scale=0.5).then_inc(gt_done, 1)

            def squash(t):
                act.wait_ge(mix_done, t + 1)
                nc.scalar.activation(tmix[:], mix[:], ACT.Tanh, scale=0.5).then_inc(tmix_done, 1)

            projected(0, 0)
            projected(1, 1)
            keep_sl(0)
            act.wait_ge(sl_bc_done, 1)
            exponentials_0(0)
            steps(act, 2, NT // 2, projected_and_last)
            round_mask(0, 0)
            steps(act, NT // 2, NT, projected_and_last)
            exponentials_0(NT - 1)
            round_mask(1, 1)
            keep_sl(NT - 1)
            act.wait_ge(sl_bc_done, NT)
            exponentials(1)

            def beside_sums(t, slot, _):
                round_mask(t + 1, 1 - slot)
                gates(t - 1)
                exponentials(t + 1)
                squash(t - 1)

            steps(act, 1, NT - 1, beside_sums)
            for t in (NT - 2, NT - 1):
                gates(t)
                squash(t)

        @block.vector
        def _(dve):
            def copy_xT(k, slot):
                dve.wait_ge(xT_made, k + 1)
                if from_tile(k, 2):
                    dve.wait_ge(proj_done, k - 1)
                nc.vector.tensor_copy(xT[:, slot].rearrange("p c i -> p (c i)"), pT[slot][:, 0:D]).then_inc(xT_copied, 1)

            def projected(k, slot):
                dve.wait_ge(hi_done, k + 1)
                nc.vector.tensor_tensor(xw_lo[:, k, :], pM[slot][:, 0:MW], xw_hi[:, k, :].bitcast(fp32),
                                        ALU.subtract).then_inc(pM_read, 1)
                dve.wait_ge(dc_done, k + 1)
                nc.vector.tensor_copy(s_own[:, k, :], pE[slot][:, D:HW]).then_inc(s_own_done, 1)
                nc.vector.tensor_scalar(hD[:, k, 0:D], pE[slot][:, 0:D], hD[:, k, D:D + 1], None,
                                        ALU.mult).then_inc(pE_read, 1)

            def copy_and_projected(k, slot, _):
                copy_xT(k + 1, 1 - slot)
                projected(k, slot)

            def transpose_adj(t, slot, half):
                dve.wait_ge(adj_arrived[slot], half * (16 * B) + 16 * B)
                if from_tile(t, 2):
                    dve.wait_ge(maskT_done, t - 1)
                nc.vector.transpose(adjT[:, slot].bitcast(u32).rearrange("p k (b s) -> p b k s", b=B),
                                    adj_in[:, slot].bitcast(u32).rearrange("p b (k r) -> p b k r", r=S)
                                    ).then_inc(adjT_done, 1)

            copy_xT(0, 0)
            dve.wait_ge(wsa_in, 32)
            n = 0
            for c in range(NC):
                for side, col in ((1, D), (0, D + 1)):
                    nc.vector.scalar_tensor_tensor(wprod[:, n, :], wsa[:, c, 0:D], SLOPE - 1.0, a_bc[:, side, :],
                                                   ALU.mult, ALU.mult).then_inc(wprod_done, 1)
                    n += 1
                    dve.wait_ge(wprod_done, n)
                    nc.vector.reduce_sum(wsa[:, c, col:col + 1], wprod[:, n - 1, :], axis=AX.X).then_inc(wcol_done, 1)

            copy_and_projected(0, 0, 0)
            copy_and_projected(1, 1, 0)
            steps(dve, 2, NT // 2 - 2, copy_and_projected)
            transpose_adj(0, 0, 0)
            steps(dve, NT // 2 - 2, NT - 1, copy_and_projected)
            transpose_adj(1, 1, 0)
            projected(NT - 1, 1)

            dve.wait_ge(maskT_done, 1)
            for g in range(NG):
                dve.wait_ge(sg0_done, G * (g + 1))
                part = slice(G * g, G * (g + 1))
                last = nc.vector.scalar_tensor_tensor(
                    eT[:, 0, part].rearrange("p k i -> p (k i)"), sg[:, part].rearrange("p k i -> p (k i)"), 1.0,
                    maskT[:, 0, part].bitcast(fp32).rearrange("p k i -> p (k i)"), ALU.min, ALU.mult)
                last.then_inc(eT0_done, 1)
            dve.wait_ge(small_in, 48)
            dve.wait_ge(s_own_done, NT)
            nc.vector.tensor_tensor(gate_own[:], s_own[:, :, 2:4],
                                    gate_bias[:].unsqueeze(1).to_broadcast([P, NT, 2]), ALU.add).then_inc(gate_own_done, 1)
            def weigh(t, slot):
                dve.wait_ge(sg_done, t)
                dve.wait_ge(maskT_done, t + 1)
                if from_tile(t, 2):
                    dve.wait_ge(att_done, t - 1)
                flat = "p k i -> p (k i)"
                nc.vector.scalar_tensor_tensor(eT[:, slot].rearrange(flat), sg[:].rearrange(flat), 1.0,
                                               maskT[:, slot].bitcast(fp32).rearrange(flat),
                                               ALU.min, ALU.mult).then_inc(eT_done, 1)

            def gate_logits(t, slot):
                dve.wait_ge(nbr_done, t + 1)
                nc.vector.tensor_tensor(gz[:], pM[slot][:, D:D + 2], gate_own[:, t, :], ALU.add).then_inc(gz_done, 1)

            def gated_neighbours(t, slot):
                dve.wait_ge(gt_done, t + 1)
                nc.vector.tensor_scalar(gate[:], gt[:], 0.5, 0.5, ALU.mult, ALU.add).then_inc(gate_done, 1)
                dve.wait_ge(gate_done, t + 1)
                nc.vector.tensor_scalar(xb_bias[:], bg_bc[:], gate[:, 1:2], None, ALU.mult).then_inc(xb_bias_done, 1)
                dve.wait_ge(xb_bias_done, t + 1)
                nc.vector.scalar_tensor_tensor(xb_gated[:], pM[slot][:, 0:D], gate[:, 1:2], xb_bias[:],
                                               ALU.mult, ALU.add).then_inc(xb_gated_done, 1)

            def mix_sums(t, slot):
                dve.wait_ge(att_done, t + 1)
                nc.vector.tensor_scalar(den[:], pE[slot][:, D:D + 1], hD[:, t, D + 1:D + 2], EPS_DEN,
                                        ALU.mult, ALU.add).then_inc(den_done, 1)
                dve.wait_ge(den_done, t + 1)
                nc.vector.reciprocal(rden[:], den[:]).then_inc(rden_done, 1)
                dve.wait_ge(rden_done, t + 1)
                nc.vector.tensor_scalar(coef[:], gate[:, 0:1], hD[:, t, D + 1:D + 2], rden[:, 0:1],
                                        ALU.mult, ALU.mult).then_inc(coef_done, 1)
                dve.wait_ge(coef_done, t + 1)
                nc.vector.scalar_tensor_tensor(mix[:], pE[slot][:, 0:D], coef[:, 0:1], xb_gated[:],
                                               ALU.mult, ALU.add).then_inc(mix_done, 1)

            def residual(t):
                dve.wait_ge(tmix_done, t + 1)
                nc.vector.scalar_tensor_tensor(res[:], tmix[:], 0.5, xs[:, t, :], ALU.mult, ALU.add).then_inc(res_done, 1)
                dve.wait_ge(res_done, t + 1)
                nc.vector.bn_stats(stats[:], res[:]).then_inc(stats_done, 1)

            def variance(t):
                nc.vector.bn_aggr(mean_var[:], stats[:]).then_inc(var_done, 1)

            def normalise(t, slot, half):
                dve.wait_ge(rstd_done, t + 1)
                if from_tile(t, 2):
                    dve.wait_ge(y_out[slot], half * 16)
                nc.vector.tensor_scalar(y[:, slot, :], res[:], mean_var[:, 0:1], rstd[:, 0:1],
                                        ALU.subtract, ALU.mult).then_inc(y_done, 1)

            transpose_adj(2, 0, 1)
            dve.wait_ge(gate_own_done, 1)
            weigh(1, 1)

            def beside_sums(t, slot, half):
                gate_logits(t - 1, 1 - slot)
                if from_tile(t, 2):
                    normalise(t - 2, slot, half - 1)
                gated_neighbours(t - 1, 1 - slot)
                mix_sums(t - 1, 1 - slot)
                if not isinstance(t, int) or t + 2 < NT:
                    transpose_adj(t + 2, slot, half + 1)
                residual(t - 1)
                dve.wait_ge(stats_done, t)
                weigh(t + 1, 1 - slot)
                variance(t - 1)

            for t in (1, 2, 3):
                beside_sums(t, t % 2, t // 2)
            steps(dve, 4, NT - 2, beside_sums)
            beside_sums(NT - 2, 0, NT // 2 - 1)
            normalise(NT - 3, 1, NT // 2 - 2)
            for t in (NT - 2, NT - 1):
                gate_logits(t, t % 2)
                gated_neighbours(t, t % 2)
                mix_sums(t, t % 2)
                residual(t)
                dve.wait_ge(stats_done, t + 1)
                variance(t)
                normalise(t, t % 2, t // 2)

        @block.tensor
        def _(pe):
            def transpose_x(k, slot):
                if from_tile(k, 2):
                    pe.wait_ge(x_slot_full, k - 1)
                    pe.wait_ge(xT_copied, k - 1)
                    tile = x_slot[:, slot, :]
                else:
                    pe.wait_ge(x_in[0], 16 * B)
                    tile = xs[:, k, :]
                for c in range(NC):
                    last = nc.tensor.transpose(pT[slot][:, c * P:(c + 1) * P], tile[:, c * P:(c + 1) * P], ident[:])
                last.then_inc(xT_made, 1)

            def project(k, slot):
                pe.wait_ge(xT_copied, k + 1)
                if from_tile(k, 2):
                    pe.wait_ge(pE_read, k - 1)
                    pe.wait_ge(pM_read, k - 1)
                for c in range(NC):
                    last = nc.tensor.matmul(pM[slot][:, 0:MW], xT[:, slot, c, :], wg[:, c, :],
                                            start=c == 0, stop=c == NC - 1)
                last.then_inc(proj_m_done, 1)
                if not from_tile(k, 1):
                    pe.wait_ge(wcol_done, 2 * NC)
                for c in range(NC):
                    last = nc.tensor.matmul(pE[slot][:, 0:HW], xT[:, slot, c, :], wsa[:, c, :], start=c == 0, stop=c == NC - 1)
                last.then_inc(proj_done, 1)

            def transpose_sl(k, slot):
                pe.wait_ge(sq_done, k + 1)
                if from_tile(k, 1):
                    pe.wait_ge(sl_bc_done, k)
                nc.tensor.transpose(pS[:, 0:P], sl_sq[:, slot, :], ident[:]).then_inc(slT_made, 1)

            def all_three(k, slot, _):
                transpose_x(k + 1, 1 - slot)
                project(k, slot)
                transpose_sl(k - 1, 1 - slot)

            def neighbour_sums(t, slot):
                pe.wait_ge(maskT_done, t + 1)
                if from_tile(t, 2):
                    pe.wait_ge(xb_gated_done, t - 1)
                for k in range(NT):
                    if isinstance(t, int) and t == 0 and k == NT - 1:
                        pe.wait_ge(hi_done, NT)
                        pe.wait_ge(pM_read, NT)
                    nc.tensor.matmul(pM[slot][:, 0:MW], maskT[:, slot, k, :], xw_hi[:, k, :], start=k == 0, stop=False)
                    last = nc.tensor.matmul(pM[slot][:, 0:MW], maskT[:, slot, k, :], xw_lo[:, k, :],
                                            start=False, stop=k == NT - 1)
                last.then_inc(nbr_done, 1)

            def attention_sums(t, slot):
                if from_tile(t, 1):
                    pe.wait_ge(eT_done, t)
                if from_tile(t, 2):
                    pe.wait_ge(mix_done, t - 1)
                for k in range(NT):
                    if isinstance(t, int) and t == 0 and k % G == 0:
                        pe.wait_ge(eT0_done, k // G + 1)
                    last = nc.tensor.matmul(pE[slot][:, 0:EW], eT[:, slot, k, :], hD[:, k, 0:EW],
                                            start=k == 0, stop=k == NT - 1)
                last.then_inc(att_done, 1)

            def beside_copies(t, slot, _):
                neighbour_sums(t, slot)
                attention_sums(t, slot)

            pe.wait_ge(const, 4)
            pe.wait_ge(rows_in, 32)
            for c in range(NC):
                last = nc.tensor.matmul(pU[:, 4 * c:4 * c + 4], gate_rows[0:4, c * P:(c + 1) * P], ident[0:4, 0:4],
                                        start=True, stop=True)
            last.then_inc(gate_cols_made, 1)
            transpose_x(0, 0)
            transpose_x(1, 1)
            pe.wait_ge(wg_in, 16)
            pe.wait_ge(gate_cols_copied, 2)
            project(0, 0)
            all_three(1, 1, 0)
            steps(pe, 2, NT - 1, all_three)
            project(NT - 1, 1)
            transpose_sl(NT - 2, 0)
            pe.wait_ge(pE_read, NT - 1)
            pe.wait_ge(pM_read, NT - 1)
            neighbour_sums(0, 0)
            transpose_sl(NT - 1, 1)
            attention_sums(0, 0)
            beside_copies(1, 1, 0)
            steps(pe, 2, NT - 1, beside_copies)
            neighbour_sums(NT - 1, 1)
            attention_sums(NT - 1, 1)


_INS = ['x', 'adj', 'L0_gnn_W_sa', 'L0_gnn_a_sa', 'L0_gnn_W_gcnb', 'L0_gnn_b_gcnb', 'L0_gnn_Wa', 'L0_gnn_ba',
        'L0_gnn_Wb', 'L0_gnn_bb']
_OUT_SHAPE, _OUT_DTYPE = (2048, 256), 'float32'


def kernel(**inputs):
    import numpy as _np
    import concourse.bacc as _bacc
    from concourse import mybir as _mybir
    from concourse.bass_utils import run_bass_kernel_spmd as _run

    nc = _bacc.Bacc("TRN2", target_bir_lowering=False, num_devices=1)
    arrays, args = {}, []
    for name in _INS:
        a = _np.ascontiguousarray(inputs[name])
        arrays[f"in_{name}_dram"] = a
        args.append(nc.dram_tensor(f"in_{name}_dram", a.shape, _mybir.dt.from_np(a.dtype), kind="ExternalInput").ap())
    args.append(nc.dram_tensor("out_dram", _OUT_SHAPE, _mybir.dt.from_np(_np.dtype(_OUT_DTYPE)),
                               kind="ExternalOutput").ap())
    gated_two_relation_gnn_kernel(nc, *args)
    r = _run(nc, [arrays], core_ids=[0])
    return r.results[0]["out_dram"]
```

```python
import concourse.bass as bass
from concourse import mybir
from contextlib import ExitStack


def gated_two_relation_gnn_kernel(
    nc: bass.Bass,
    x: bass.AP,
    adj: bass.AP,
    W_sa: bass.AP,
    a_sa: bass.AP,
    W_g: bass.AP,
    b_g: bass.AP,
    Wa: bass.AP,
    ba: bass.AP,
    Wb: bass.AP,
    bb: bass.AP,
    out: bass.AP,
):
    fp32 = mybir.dt.float32
    f32r = mybir.dt.float32r
    bf16 = mybir.dt.bfloat16
    u32 = mybir.dt.uint32
    i32 = mybir.dt.int32
    ALU = mybir.AluOpType
    ACT = mybir.ActivationFunctionType
    AX = mybir.AxisListType

    P = 128
    N, D = x.shape
    NT = N // P
    NC = D // P
    S = 32
    B = P // S
    NG = 4
    G = NT // NG
    TURN = S // 4
    FIRST = 4
    LATE = NT // 2 - 1
    WARM_UP = 8
    EW = D + 1
    MW = D + 2
    HW = D + 4
    LEFT, RIGHT = slice(0, D // 2), slice(D // 2, D)
    SLOPE = 0.01
    EPS_DEN, EPS_LN = 1e-05, 1e-05

    x_v = x.rearrange("(b k s) d -> b s k d", b=B, s=S)
    x_quarters_v = x.rearrange("(b k s) (a f) -> a b s k f", b=B, s=S, a=B)
    adj_v = adj.rearrange("(b t s) (a n) -> t a s b n", b=B, s=S, a=B)
    out_v = out.rearrange("(b t s) d -> t b s d", b=B, s=S)

    sl_rows = nc.dram_tensor("sl_rows", [NT, P], fp32, kind="Internal").ap()

    ctx = ExitStack()
    with ctx:
        def sb(name, shape, dt=fp32):
            return ctx.enter_context(nc.sbuf_tensor(name, shape, dt))

        def pb(name):
            return ctx.enter_context(nc.psum_tensor(name, [P, 512], fp32))

        def sem(name):
            return ctx.enter_context(nc.semaphore(name))

        xs = sb("xs", [P, NT, D])
        x_quarters = sb("x_quarters", [P, B, NT - LATE, D // B])
        wsa = sb("wsa", [P, NC, HW])
        wg = sb("wg", [P, NC, MW])
        gate_cols = sb("gate_cols", [P, 2, 2, NC])
        a_bc = sb("a_bc", [P, 2 * D])
        bg_bc = sb("bg_bc", [P, D])
        gate_bias = sb("gate_bias", [P, 2])
        adj_in = sb("adj_in", [P, 2, B, N // B])
        ident = sb("ident", [P, P])
        ones = sb("ones", [P, P])
        eps = sb("eps", [P, 1])
        minus_half = sb("minus_half", [P, 1])
        scratch = sb("scratch", [P, 1])
        x_slot = sb("x_slot", [P, 2, NC, P])
        xT = sb("xT", [P, 2, NC, P])
        hD = sb("hD", [P, NT, EW + 1])
        xw_hi = sb("xw_hi", [P, NT, MW], f32r)
        xw_lo = sb("xw_lo", [P, NT, MW], f32r)
        s_own = sb("s_own", [P, NT, 4])
        gate_own = sb("gate_own", [P, NT, 2])
        wprod = sb("wprod", [P, 2 * NC, D])
        sl_sq = sb("sl_sq", [P, P])
        own_turned = sb("own_turned", [P, NT // TURN, S])
        sl_bc = sb("sl_bc", [P, NT, P])
        adjT = sb("adjT", [P, 2, NT, P])
        maskT = sb("maskT", [P, 2, NT, P], f32r)
        sg = sb("sg", [P, 2, NT, P])
        is_other = sb("is_other", [P, NT * P], bf16)
        others = sb("others", [P, NG + NT - 1, 1])
        others_sum = sb("others_sum", [P, 1])
        general = sb("general", [1, 1], i32)
        eT = sb("eT", [P, 2, NT, P])
        gz = sb("gz", [P, 2])
        gt = sb("gt", [P, 2])
        gate = sb("gate", [P, 2])
        den = sb("den", [P, 1])
        rden = sb("rden", [P, 1])
        coef = sb("coef", [P, 1])
        xb_bias = sb("xb_bias", [P, D])
        xb_gated = sb("xb_gated", [P, D])
        mix = sb("mix", [P, D])
        tmix = sb("tmix", [P, D])
        res = sb("res", [P, D])
        stats = sb("stats", [P, 2, 6])
        mean_var = sb("mean_var", [P, 2])
        var_eps = sb("var_eps", [P, 1])
        rstd = sb("rstd", [P, 1])
        y = sb("y", [P, 2, D])

        pT = [pb("pT0"), pb("pT1")]
        pE = [pb("pE0"), pb("pE1")]
        pM = [pb("pM0"), pb("pM1")]
        pS = pb("pS")

        x_in = [sem("x_in0"), sem("x_in1"), sem("x_in_late")]
        x_quarters_in = sem("x_quarters_in")
        gate_cols_in = sem("gate_cols_in")
        gate_cols_copied = sem("gate_cols_copied")
        wsa_in = sem("wsa_in")
        a_in = sem("a_in")
        wg_in = sem("wg_in")
        small_in = sem("small_in")
        adj_arrived = [sem("adj_arrived0"), sem("adj_arrived1")]
        zeros_set = sem("zeros_set")
        ones_set = sem("ones_set")
        const = sem("const")
        wcol_done = sem("wcol_done")
        x_slot_full = sem("x_slot_full")
        xT_made = sem("xT_made")
        xT_done = sem("xT_done")
        proj_m_done = sem("proj_m_done")
        proj_done = sem("proj_done")
        dc_done = sem("dc_done")
        gate_own_done = sem("gate_own_done")
        hi_done = sem("hi_done")
        s_own_done = sem("s_own_done")
        sq_done = sem("sq_done")
        pE_read = sem("pE_read")
        pM_read = sem("pM_read")
        slT_made = sem("slT_made")
        sl_bc_done = sem("sl_bc_done")
        own_turned_done = sem("own_turned_done")
        sl_out = [sem(f"sl_out{n}") for n in range(NT // TURN)]
        sl_in = [sem(f"sl_in{n}") for n in range(NT // TURN)]
        adjT0_done = sem("adjT0_done")
        adjT_done = sem("adjT_done")
        maskT0_done = sem("maskT0_done")
        maskT_done = sem("maskT_done")
        sg_done = sem("sg_done")
        sg0_done = sem("sg0_done")
        eT0_done = sem("eT0_done")
        eT_done = sem("eT_done")
        nbr_done = sem("nbr_done")
        att_done = sem("att_done")
        right_summed = sem("right_summed")
        right_mixed = sem("right_mixed")
        right_squashed = sem("right_squashed")
        right_res_done = sem("right_res_done")
        gz_done = sem("gz_done")
        gt_done = sem("gt_done")
        gate_done = sem("gate_done")
        den_done = sem("den_done")
        rden_done = sem("rden_done")
        coef_done = sem("coef_done")
        xb_bias_done = sem("xb_bias_done")
        xb_gated_done = sem("xb_gated_done")
        mix_done = sem("mix_done")
        tmix_done = sem("tmix_done")
        res_done = sem("res_done")
        stats_done = sem("stats_done")
        var_done = sem("var_done")
        var_eps_done = sem("var_eps_done")
        rstd_done = sem("rstd_done")
        y_done = sem("y_done")
        checked = sem("checked")
        others_summed = sem("others_summed")
        others_added = sem("others_added")
        general_set = sem("general_set")
        sg_min_done = sem("sg_min_done")
        y_out = [sem("y_out0"), sem("y_out1")]

        block = ctx.enter_context(nc.Block())

        def steps(eng, first, last, body):
            pairs = max(last - first, 0) // 2
            if pairs > 1:
                with eng.Fori(0, pairs) as r:
                    for t in (first, first + 1):
                        body(r * 2 + t, t % 2, r + t // 2)
            else:
                for t in range(first, first + 2 * pairs):
                    body(t, t % 2, t // 2)
            if first < last and (last - first) % 2:
                body(last - 1, (last - 1) % 2, (last - 1) // 2)

        def from_tile(t, n):
            return not isinstance(t, int) or t >= n

        def verdict(eng):
            eng.wait_ge(general_set, 1)
            return eng.value_load(general[0:1, 0:1], min_val=0, max_val=1)

        def second_pass(eng, body):
            with eng.If(verdict(eng)):
                body(NT)

        @block.sync
        def _(sp):
            def load_x(first, last, arrived):
                for b in range(B):
                    sp.dma_start(xs[S * b:S * (b + 1), first:last, :], x_v[b, :, first:last, :]).then_inc(arrived, 16)

            def load_x_quarters():
                for a in range(B):
                    for b in range(B):
                        sp.dma_start(x_quarters[S * a:S * (a + 1), b, :, :],
                                     x_quarters_v[a, b, :, LATE:, :]).then_inc(x_quarters_in, 16)

            def load(t, slot):
                for a in range(B):
                    sp.dma_start(adj_in[S * a:S * (a + 1), slot, :, :],
                                 adj_v[t, a]).then_inc(adj_arrived[slot], 16)

            def store(t, slot, past=0):
                sp.wait_ge(y_done, t + (past + 1))
                sp.dma_start(out_v[t], y[:, slot, :]).then_inc(y_out[slot], 16)

            def load_ahead(t, slot, _):
                if from_tile(t, 1):
                    sp.wait_ge(adjT_done, t)
                else:
                    sp.wait_ge(adjT0_done, NG)
                load(t + 2, slot)
                if from_tile(t, 2):
                    store(t - 2, slot)

            def spread_sl(n):
                sp.wait_ge(own_turned_done, n + 1)
                sp.dma_start(sl_rows[TURN * n:TURN * (n + 1), :].rearrange("k (b s) -> b k s", b=B),
                             own_turned[1:P:4, n, :]).then_inc(sl_out[n], 16)
                sp.wait_ge(sl_out[n], 16)
                tiles = slice(max(TURN * n, 1), TURN * (n + 1))
                row = sl_rows[tiles, :].rearrange("(o k) i -> o (k i)", o=1)
                sp.dma_start(sl_bc[:, tiles, :].rearrange("p k i -> p (k i)"),
                             row.to_broadcast([P, (tiles.stop - tiles.start) * P])).then_inc(sl_in[n], 16)

            load_x(0, FIRST, x_in[0])
            sp.dma_start(wg[:, :, 0:D], W_g.rearrange("(p c) n -> p c n", c=NC)).then_inc(wg_in, 16)
            sp.dma_start(wsa[:, :, 0:D], W_sa.rearrange("(p c) n -> p c n", c=NC)).then_inc(wsa_in, 16)
            load_x(FIRST, LATE, x_in[1])
            load(0, 0)
            load_x_quarters()
            load_x(LATE, NT, x_in[2])
            load(1, 1)
            spread_sl(0)
            load_ahead(0, 0, 0)
            spread_sl(1)
            load_ahead(1, 1, 0)
            steps(sp, 2, NT - 2, load_ahead)
            for t in range(NT - 4, NT - 1):
                store(t, t % 2)
            adj_is_general = verdict(sp)
            store(NT - 1, 1)
            for slot in range(2):
                sp.wait_ge(y_out[slot], 16 * (NT // 2))

            def load_and_store(past):
                load(0, 0)

                def one_tile(t, slot, _):
                    sp.wait_ge(adjT_done, t + past)
                    load(t + 1, 1 - slot)
                    store(t, slot, past)

                steps(sp, 0, NT - 1, one_tile)
                store(NT - 1, 1, past)
                for slot in range(2):
                    sp.wait_ge(y_out[slot], 16 * NT)

            with sp.If(adj_is_general):
                load_and_store(NT)

        @block.gpsimd
        def _(pool):
            nc.gpsimd.memset(ones[:], 1.0).then_inc(ones_set, 1)
            for n, w in enumerate((Wa, Wb)):
                pool.dma_start(gate_cols[:, n], w.rearrange("o (h p c) -> p (o h) c", h=2, c=NC)).then_inc(gate_cols_in, 16)
            pool.dma_start(a_bc[:], a_sa.to_broadcast([P, 2 * D])).then_inc(a_in, 16)
            nc.gpsimd.memset(ident[:], 0.0).then_inc(zeros_set, 1)
            pool.wait_ge(zeros_set, 1)
            nc.gpsimd.affine_select(out=ident[:], in_=ident[:], compare_op=ALU.not_equal, fill=1.0,
                                    base=0, pattern=[[-1, P]], channel_multiplier=1).then_inc(const, 1)
            nc.gpsimd.memset(eps[:], EPS_LN).then_inc(const, 1)
            nc.gpsimd.memset(minus_half[:], -0.5).then_inc(const, 1)

            def fill_slot(k, slot):
                if from_tile(k, 4):
                    pool.wait_ge(xT_made, k - 1)
                nc.gpsimd.tensor_copy(x_slot[:, slot], xs[:, k].rearrange("p (n c) -> p c n", c=NC)).then_inc(x_slot_full, 1)

            pool.wait_ge(x_in[0], 16 * B)
            fill_slot(2, 0)
            fill_slot(3, 1)
            pool.dma_start(bg_bc[:], b_g.rearrange("(o n) -> o n", o=1).to_broadcast([P, D])).then_inc(small_in, 16)
            pool.dma_start(gate_bias[:, 0:1], ba.rearrange("(o n) -> o n", o=1).to_broadcast([P, 1])).then_inc(small_in, 16)
            pool.dma_start(gate_bias[:, 1:2], bb.rearrange("(o n) -> o n", o=1).to_broadcast([P, 1])).then_inc(small_in, 16)
            pool.wait_ge(ones_set, 1)
            pool.wait_ge(s_own_done, 1)
            nc.gpsimd.tensor_tensor(sl_sq[:], ones[:], s_own[:, 0, 1:2].to_broadcast([P, P]), ALU.mult).then_inc(sq_done, 1)
            pool.wait_ge(x_in[1], 16 * B)
            for k in range(FIRST, LATE):
                fill_slot(k, k % 2)
            pool.wait_ge(const, 3)

            def inverse_deviation(t, slot, half, past=0):
                pool.wait_ge(var_done, t + (past + 1))
                nc.gpsimd.tensor_tensor(var_eps[:], mean_var[:, 1:2], eps[:], ALU.add).then_inc(var_eps_done, 1)
                pool.wait_ge(var_eps_done, t + (past + 1))
                nc.gpsimd.tensor_tensor(rstd[:], var_eps[:], minus_half[:], ALU.pow).then_inc(rstd_done, 1)

            steps(pool, 0, NT, inverse_deviation)
            second_pass(pool, lambda past: steps(pool, 0, NT, lambda t, slot, half: inverse_deviation(t, slot, half, past)))

        @block.scalar
        def _(act):
            act.wait_ge(gate_cols_in, 32)
            nc.scalar.activation(wg[:, :, D:D + 2], gate_cols[:, :, 0, :].rearrange("p n c -> p c n"),
                                 ACT.Copy).then_inc(gate_cols_copied, 1)
            nc.scalar.activation(wsa[:, :, D + 2:D + 4], gate_cols[:, :, 1, :].rearrange("p n c -> p c n"),
                                 ACT.Copy).then_inc(gate_cols_copied, 1)
            act.wait_ge(const, 3)
            nc.scalar.activation(scratch[:], eps[:], ACT.Exp)

            def projected(k, slot):
                act.wait_ge(proj_m_done, k + 1)
                nc.scalar.activation(xw_hi[:, k, :], pM[slot][:, 0:MW], ACT.Copy).then_inc(hi_done, 1)
                act.wait_ge(proj_done, k + 1)
                nc.scalar.activation(hD[:, k, D:D + 2], pE[slot][:, D:D + 2], ACT.Exp,
                                     scale=SLOPE / (1.0 - SLOPE)).then_inc(dc_done, 1)

            def exponentials_0(k):
                act.wait_ge(s_own_done, k + 1)
                nc.scalar.activation(sg[:, 0, k, :], sl_bc[:, 0, :], ACT.Exp, bias=s_own[:, k, 0:1]).then_inc(sg0_done, 1)

            def projected_and_last(k, slot, _):
                projected(k, slot)
                exponentials_0(k - 1)

            def round_mask(t, slot):
                act.wait_ge(adjT_done, t)
                if from_tile(t, 2):
                    act.wait_ge(att_done, t - 1)
                nc.scalar.activation(maskT[:, slot].rearrange("p k i -> p (k i)"),
                                     adjT[:, slot].rearrange("p k i -> p (k i)"), ACT.Copy).then_inc(maskT_done, 1)

            def exponentials(t, slot, past=0):
                if past or from_tile(t, 3):
                    act.wait_ge(eT_done, t + (past - 2))
                elif t == 2:
                    act.wait_ge(eT0_done, NG)
                for k in range(NT):
                    last = nc.scalar.activation(sg[:, slot, k, :], sl_bc[:, t, :], ACT.Exp, bias=s_own[:, k, 0:1])
                last.then_inc(sg_done, 1)

            def gates(t, past=0):
                act.wait_ge(gz_done, t + (past + 1))
                nc.scalar.activation(gt[:], gz[:], ACT.Tanh, scale=0.5).then_inc(gt_done, 1)
                act.wait_ge(gate_done, t + (past + 1))
                nc.scalar.activation(xb_bias[:], bg_bc[:], ACT.Copy, scale=gate[:, 1:2]).then_inc(xb_bias_done, 1)

            def squash(t, past=0, cols=slice(0, D)):
                act.wait_ge(mix_done, t + (past + 1))
                nc.scalar.activation(tmix[:, cols], mix[:, cols], ACT.Tanh, scale=0.5).then_inc(tmix_done, 1)

            projected(0, 0)
            projected(1, 1)
            projected(2, 0)
            act.wait_ge(slT_made, 1)
            nc.scalar.activation(sl_bc[:, 0, :], pS[:, 0:P], ACT.Copy).then_inc(sl_bc_done, 1)
            act.wait_ge(sl_bc_done, 1)
            exponentials_0(0)
            exponentials_0(1)
            projected_and_last(3, 1, 1)
            projected_and_last(4, 0, 2)
            for g in range(NG):
                act.wait_ge(adjT0_done, g + 1)
                part = slice(G * g, G * (g + 1))
                nc.scalar.activation(maskT[:, 0, part].rearrange("p k i -> p (k i)"),
                                     adjT[:, 0, part].rearrange("p k i -> p (k i)"), ACT.Copy).then_inc(maskT0_done, 1)
                steps(act, G * (g + 1) + 1, min(G * (g + 2) + 1, NT), projected_and_last)
            exponentials_0(NT - 1)
            act.wait_ge(sl_in[0], 16)
            exponentials(1, 1)
            round_mask(1, 1)
            exponentials(2, 0)
            act.wait_ge(sl_in[1], 16)

            def beside_sums(t, slot, _):
                gates(t - 1)
                round_mask(t + 1, 1 - slot)
                squash(t - 1)
                exponentials(t + 2, slot)

            steps(act, 1, NT - 2, beside_sums)
            gates(NT - 3)
            round_mask(NT - 1, 1)
            squash(NT - 3)
            gates(NT - 2)
            squash(NT - 2)
            gates(NT - 1)
            act.wait_ge(right_mixed, 1)
            nc.scalar.activation(tmix[:, RIGHT], mix[:, RIGHT], ACT.Tanh, scale=0.5).then_inc(right_squashed, 1)
            squash(NT - 1, cols=LEFT)

            def functions(past):
                def one_tile(t, slot, _):
                    exponentials(t, slot, past)
                    gates(t, past)
                    squash(t, past)

                steps(act, 0, NT, one_tile)

            second_pass(act, functions)

        @block.vector
        def _(dve):
            def copy_xT(k, slot):
                dve.wait_ge(xT_made, k + 1)
                if from_tile(k, 2):
                    dve.wait_ge(proj_done, k - 1)
                nc.vector.tensor_copy(xT[:, slot].rearrange("p c i -> p (c i)"), pT[slot][:, 0:D]).then_inc(xT_done, 1)

            def transpose_x(k, slot):
                dve.wait_ge(proj_done, k - 1)
                nc.vector.transpose(xT[:, slot].bitcast(u32).rearrange("p c (b s) -> p b c s", b=B),
                                    x_quarters[:, :, k - LATE].bitcast(u32).rearrange("p b (r c) -> p b c r", c=NC)
                                    ).then_inc(xT_done, 1)

            def projected_m(k, slot):
                dve.wait_ge(hi_done, k + 1)
                nc.vector.tensor_tensor(xw_lo[:, k, :], pM[slot][:, 0:MW], xw_hi[:, k, :].bitcast(fp32),
                                        ALU.subtract).then_inc(pM_read, 1)

            def projected_e(k, slot):
                dve.wait_ge(dc_done, k + 1)
                nc.vector.tensor_copy(s_own[:, k, :], pE[slot][:, D:HW]).then_inc(s_own_done, 1)
                nc.vector.tensor_scalar(hD[:, k, 0:D], pE[slot][:, 0:D], hD[:, k, D:D + 1], None,
                                        ALU.mult).then_inc(pE_read, 1)

            def turn_own(n):
                dve.wait_ge(s_own_done, TURN * (n + 1))
                nc.vector.transpose(own_turned[:, n, :].bitcast(u32),
                                    s_own[:, TURN * n:TURN * (n + 1), :].bitcast(u32).rearrange("p k n -> p (k n)")
                                    ).then_inc(own_turned_done, 1)

            def transpose_part(g):
                part = slice(G * g, G * (g + 1))
                nc.vector.transpose(adjT[:, 0, part].bitcast(u32).rearrange("p k (b s) -> p b k s", b=B),
                                    adj_in[:, 0, :, S * G * g:S * G * (g + 1)].bitcast(u32)
                                    .rearrange("p b (k r) -> p b k r", r=S)).then_inc(adjT0_done, 1)

            def check_part(g):
                dve.wait_ge(adjT0_done, g + 1)
                part = adjT[:, 0, G * g:G * (g + 1)].rearrange("p k i -> p (k i)")
                nc.vector.scalar_tensor_tensor(is_other[:, P * G * g:P * G * (g + 1)], part, 0.0, part,
                                               ALU.not_equal, ALU.not_equal,
                                               accum_out=others[:, g, :]).then_inc(checked, 1)

            def transpose_adj(t, slot, half, past=0):
                dve.wait_ge(adj_arrived[slot], half * (16 * B) + 16 * B * (past // 2 + 1))
                if past:
                    dve.wait_ge(nbr_done, t + (past - 1))
                elif from_tile(t, 2):
                    dve.wait_ge(checked, t + (NG - 2))
                if not past and from_tile(t, 3):
                    dve.wait_ge(maskT_done, t - 2)
                nc.vector.transpose(adjT[:, slot].bitcast(u32).rearrange("p k (b s) -> p b k s", b=B),
                                    adj_in[:, slot].bitcast(u32).rearrange("p b (k r) -> p b k r", r=S)
                                    ).then_inc(adjT_done, 1)

            copy_xT(0, 0)
            copy_xT(1, 1)
            dve.wait_ge(wsa_in, 16)
            dve.wait_ge(a_in, 16)
            for c in range(NC):
                for side, col in ((1, D), (0, D + 1)):
                    nc.vector.scalar_tensor_tensor(wprod[:, 2 * c + side, :], wsa[:, c, 0:D], SLOPE - 1.0,
                                                   a_bc[:, side * D:(side + 1) * D], ALU.mult, ALU.mult,
                                                   accum_out=wsa[:, c, col:col + 1]).then_inc(wcol_done, 1)

            projected_m(0, 0)
            for k in range(1, NT):
                if k + 1 < LATE:
                    copy_xT(k + 1, (k + 1) % 2)
                elif k + 1 < NT:
                    if k + 1 == LATE:
                        dve.wait_ge(x_quarters_in, 16 * B * B)
                    transpose_x(k + 1, (k + 1) % 2)
                projected_e(k - 1, (k - 1) % 2)
                part = k // G - 1
                if k == TURN:
                    turn_own(0)
                if k == G:
                    dve.wait_ge(adj_arrived[0], 16 * B)
                if k == NT - 1:
                    transpose_part(NG - 1)
                elif part >= 0 and k % G == 0:
                    transpose_part(part)
                elif part >= 0 and k % G == 2:
                    check_part(part)
                projected_m(k, k % 2)
            projected_e(NT - 1, 1)
            turn_own(1)
            check_part(NG - 1)

            for g in range(NG):
                dve.wait_ge(sg0_done, G * (g + 1))
                dve.wait_ge(maskT0_done, g + 1)
                part = slice(G * g, G * (g + 1))
                nc.vector.scalar_tensor_tensor(
                    eT[:, 0, part].rearrange("p k i -> p (k i)"), sg[:, 0, part].rearrange("p k i -> p (k i)"), 1.0,
                    maskT[:, 0, part].bitcast(fp32).rearrange("p k i -> p (k i)"), ALU.min, ALU.mult).then_inc(eT0_done, 1)
            for part in x_in:
                dve.wait_ge(part, 16 * B)
            dve.wait_ge(small_in, 48)
            dve.wait_ge(s_own_done, NT)
            nc.vector.tensor_tensor(gate_own[:], s_own[:, :, 2:4],
                                    gate_bias[:].unsqueeze(1).to_broadcast([P, NT, 2]), ALU.add).then_inc(gate_own_done, 1)

            def check(t, slot):
                dve.wait_ge(adjT_done, t)
                dve.wait_ge(checked, t + (NG - 1))
                flat = adjT[:, slot].rearrange("p k i -> p (k i)")
                nc.vector.scalar_tensor_tensor(is_other[:], flat, 0.0, flat, ALU.not_equal, ALU.not_equal,
                                               accum_out=others[:, t + (NG - 1), :]).then_inc(checked, 1)

            def weigh(t, slot):
                dve.wait_ge(sg_done, t)
                dve.wait_ge(maskT_done, t)
                if from_tile(t, 2):
                    dve.wait_ge(att_done, t - 1)
                flat = "p k i -> p (k i)"
                nc.vector.scalar_tensor_tensor(eT[:, slot].rearrange(flat), sg[:, slot].rearrange(flat), 1.0,
                                               maskT[:, slot].bitcast(fp32).rearrange(flat),
                                               ALU.min, ALU.mult).then_inc(eT_done, 1)

            def gate_logits(t, slot, past=0):
                dve.wait_ge(nbr_done, t + (past + 1))
                nc.vector.tensor_tensor(gz[:], pM[slot][:, D:D + 2], gate_own[:, t, :], ALU.add).then_inc(gz_done, 1)

            def gates(t, past=0):
                dve.wait_ge(gt_done, t + (past + 1))
                nc.vector.tensor_scalar(gate[:], gt[:], 0.5, 0.5, ALU.mult, ALU.add).then_inc(gate_done, 1)
                dve.wait_ge(gate_done, t + (past + 1))

            def gated_neighbours(t, slot, past=0):
                dve.wait_ge(xb_bias_done, t + (past + 1))
                nc.vector.scalar_tensor_tensor(xb_gated[:], pM[slot][:, 0:D], gate[:, 1:2], xb_bias[:],
                                               ALU.mult, ALU.add).then_inc(xb_gated_done, 1)

            def attention_coef(t, slot, past=0):
                nc.vector.tensor_scalar(den[:], pE[slot][:, D:D + 1], hD[:, t, D + 1:D + 2], EPS_DEN,
                                        ALU.mult, ALU.add).then_inc(den_done, 1)
                dve.wait_ge(den_done, t + (past + 1))
                nc.vector.reciprocal(rden[:], den[:]).then_inc(rden_done, 1)
                dve.wait_ge(rden_done, t + (past + 1))
                nc.vector.tensor_scalar(coef[:], gate[:, 0:1], hD[:, t, D + 1:D + 2], rden[:, 0:1],
                                        ALU.mult, ALU.mult).then_inc(coef_done, 1)
                dve.wait_ge(coef_done, t + (past + 1))

            def mix_sums(t, slot, past=0):
                dve.wait_ge(att_done, t + (past + 1))
                attention_coef(t, slot, past)
                gated_neighbours(t, slot, past)
                dve.wait_ge(xb_gated_done, t + (past + 1))
                nc.vector.scalar_tensor_tensor(mix[:], pE[slot][:, 0:D], coef[:, 0:1], xb_gated[:],
                                               ALU.mult, ALU.add).then_inc(mix_done, 1)

            def residual(t, past=0):
                dve.wait_ge(tmix_done, t + (past + 1))
                nc.vector.scalar_tensor_tensor(res[:], tmix[:], 0.5, xs[:, t, :], ALU.mult, ALU.add).then_inc(res_done, 1)
                dve.wait_ge(res_done, t + (past + 1))
                nc.vector.bn_stats(stats[:, 0, :], res[:]).then_inc(stats_done, 1)

            def last_in_halves(t):
                dve.wait_ge(right_summed, 1)
                attention_coef(t, 1)
                nc.vector.scalar_tensor_tensor(mix[:, RIGHT], pE[1][:, RIGHT], coef[:, 0:1], xb_gated[:, RIGHT],
                                               ALU.mult, ALU.add).then_inc(right_mixed, 1)
                dve.wait_ge(right_squashed, 1)
                nc.vector.scalar_tensor_tensor(res[:, RIGHT], tmix[:, RIGHT], 0.5, xs[:, t, RIGHT],
                                               ALU.mult, ALU.add).then_inc(right_res_done, 1)
                dve.wait_ge(right_res_done, 1)
                nc.vector.bn_stats(stats[:, 1, :], res[:, RIGHT])
                dve.wait_ge(att_done, t + 1)
                nc.vector.scalar_tensor_tensor(mix[:, LEFT], pE[0][:, LEFT], coef[:, 0:1], xb_gated[:, LEFT],
                                               ALU.mult, ALU.add).then_inc(mix_done, 1)
                dve.wait_ge(tmix_done, t + 1)
                nc.vector.scalar_tensor_tensor(res[:, LEFT], tmix[:, LEFT], 0.5, xs[:, t, LEFT],
                                               ALU.mult, ALU.add).then_inc(res_done, 1)
                dve.wait_ge(res_done, t + 1)
                nc.vector.bn_stats(stats[:, 0, :], res[:, LEFT]).then_inc(stats_done, 1)

            def variance(halves=1):
                nc.vector.bn_aggr(mean_var[:], stats[:, 0:halves, :].rearrange("p h n -> p (h n)")).then_inc(var_done, 1)

            def normalise(t, slot, half, past=0):
                dve.wait_ge(rstd_done, t + (past + 1))
                if past or from_tile(t, 2):
                    dve.wait_ge(y_out[slot], half * 16 + 8 * past)
                nc.vector.tensor_scalar(y[:, slot, :], res[:], mean_var[:, 0:1], rstd[:, 0:1],
                                        ALU.subtract, ALU.mult).then_inc(y_done, 1)

            transpose_adj(1, 1, 0)
            dve.wait_ge(adjT0_done, NG)
            transpose_adj(2, 0, 1)
            dve.wait_ge(gate_own_done, 1)
            weigh(1, 1)
            check(1, 1)

            def beside_sums(t, slot, half):
                gate_logits(t - 1, 1 - slot)
                if from_tile(t, 2):
                    normalise(t - 2, slot, half - 1)
                gates(t - 1)
                mix_sums(t - 1, 1 - slot)
                if not isinstance(t, int) or t + 2 < NT:
                    transpose_adj(t + 2, slot, half + 1)
                residual(t - 1)
                dve.wait_ge(stats_done, t)
                check(t + 1, 1 - slot)
                variance()
                weigh(t + 1, 1 - slot)

            for t in (1, 2, 3):
                beside_sums(t, t % 2, t // 2)
            steps(dve, 4, NT - 2, beside_sums)
            beside_sums(NT - 2, 0, NT // 2 - 1)
            normalise(NT - 3, 1, NT // 2 - 2)
            dve.wait_ge(checked, NG + NT - 1)
            nc.vector.reduce_sum(others_sum[:], others[:, :, 0], axis=AX.X).then_inc(others_summed, 1)
            gate_logits(NT - 2, 0)
            gates(NT - 2)
            mix_sums(NT - 2, 0)
            residual(NT - 2)
            dve.wait_ge(stats_done, NT - 1)
            variance()
            normalise(NT - 2, 0, NT // 2 - 1)
            dve.wait_ge(others_added, 1)
            nc.vector.tensor_scalar(general[:], pS[0:1, 0:1], 0.0, None, ALU.is_gt).then_inc(general_set, 1)
            gate_logits(NT - 1, 1)
            gates(NT - 1)
            gated_neighbours(NT - 1, 1)
            last_in_halves(NT - 1)
            dve.wait_ge(stats_done, NT)
            variance(halves=2)
            normalise(NT - 1, 1, NT // 2 - 1)

            def weigh_any(t, slot, past):
                dve.wait_ge(sg_done, t + past)
                flat = "p k i -> p (k i)"
                nc.vector.tensor_scalar(sg[:, slot].rearrange(flat), sg[:, slot].rearrange(flat), 1.0, None,
                                        ALU.min).then_inc(sg_min_done, 1)
                dve.wait_ge(sg_min_done, t + 1)
                dve.wait_ge(adjT_done, t + past)
                dve.wait_ge(att_done, t + (past - 1))
                nc.vector.scalar_tensor_tensor(eT[:, slot].rearrange(flat), adjT[:, slot].rearrange(flat), 0.0,
                                               sg[:, slot].rearrange(flat), ALU.not_equal, ALU.mult).then_inc(eT_done, 1)

            def whole_tiles(past):
                dve.wait_ge(maskT_done, NT - 1)
                transpose_adj(0, 0, 0, past)

                def one_tile(t, slot, half):
                    weigh_any(t, slot, past)
                    gate_logits(t, slot, past)
                    gates(t, past)
                    mix_sums(t, slot, past)
                    residual(t, past)
                    dve.wait_ge(stats_done, t + (past + 1))
                    if not isinstance(t, int) or t + 1 < NT:
                        transpose_adj(t + 1, 1 - slot, half + slot, past)
                    variance()
                    normalise(t, slot, half, past)

                steps(dve, 0, NT - 2, one_tile)
                one_tile(NT - 2, 0, NT // 2 - 1)
                one_tile(NT - 1, 1, NT // 2 - 1)

            second_pass(dve, whole_tiles)

        @block.tensor
        def _(pe):
            def transpose_x(k, slot):
                if k >= 2:
                    pe.wait_ge(x_slot_full, k - 1)
                    pe.wait_ge(xT_done, k - 1)
                    tile = x_slot[:, slot]
                else:
                    pe.wait_ge(x_in[0], 16 * B)
                    tile = xs[:, k].rearrange("p (n c) -> p c n", c=NC)
                for c in range(NC):
                    last = nc.tensor.transpose(pT[slot][:, c * P:(c + 1) * P], tile[:, c, :], ident[:])
                last.then_inc(xT_made, 1)

            def project_m(k, slot):
                pe.wait_ge(xT_done, k + 1)
                if from_tile(k, 2):
                    pe.wait_ge(pM_read, k - 1)
                for c in range(NC):
                    last = nc.tensor.matmul(pM[slot][:, 0:MW], xT[:, slot, c, :], wg[:, c, :],
                                            start=c == 0, stop=c == NC - 1)
                last.then_inc(proj_m_done, 1)

            def project_e(k, slot):
                if from_tile(k, 2):
                    pe.wait_ge(pE_read, k - 1)
                elif k == 0:
                    pe.wait_ge(wsa_in, 16)
                    pe.wait_ge(wcol_done, 2 * NC)
                for c in range(NC):
                    last = nc.tensor.matmul(pE[slot][:, 0:HW], xT[:, slot, c, :], wsa[:, c, :],
                                            start=c == 0, stop=c == NC - 1)
                last.then_inc(proj_done, 1)

            def project(k, slot):
                project_m(k, slot)
                project_e(k, slot)

            def neighbour_sums(t, slot):
                if from_tile(t, 1):
                    pe.wait_ge(maskT_done, t)
                if from_tile(t, 2):
                    pe.wait_ge(xb_gated_done, t - 1)
                for k in range(NT):
                    if isinstance(t, int) and t == 0 and k % G == 0:
                        pe.wait_ge(maskT0_done, k // G + 1)
                    if isinstance(t, int) and t == 0 and k == NT - 1:
                        pe.wait_ge(hi_done, NT)
                        pe.wait_ge(pM_read, NT)
                    nc.tensor.matmul(pM[slot][:, 0:MW], maskT[:, slot, k, :], xw_hi[:, k, :], start=k == 0, stop=False)
                    last = nc.tensor.matmul(pM[slot][:, 0:MW], maskT[:, slot, k, :], xw_lo[:, k, :],
                                            start=False, stop=k == NT - 1)
                last.then_inc(nbr_done, 1)

            def attention_sums(t, slot):
                if from_tile(t, 1):
                    pe.wait_ge(eT_done, t)
                if from_tile(t, 2):
                    pe.wait_ge(mix_done, t - 1)
                for k in range(NT):
                    if isinstance(t, int) and t == 0 and k % G == 0:
                        pe.wait_ge(eT0_done, k // G + 1)
                    last = nc.tensor.matmul(pE[slot][:, 0:EW], eT[:, slot, k, :], hD[:, k, 0:EW],
                                            start=k == 0, stop=k == NT - 1)
                last.then_inc(att_done, 1)

            def beside_copies(t, slot, _):
                neighbour_sums(t, slot)
                attention_sums(t, slot)

            def keep_warm(n):
                for _ in range(n):
                    nc.tensor.matmul(pS[:, 0:P], ones[:], ones[:], start=True, stop=True)

            pe.wait_ge(ones_set, 1)
            keep_warm(WARM_UP)
            pe.wait_ge(const, 3)
            transpose_x(0, 0)
            transpose_x(1, 1)
            keep_warm(1)
            pe.wait_ge(wg_in, 16)
            pe.wait_ge(gate_cols_copied, 2)
            project_m(0, 0)
            transpose_x(2, 0)
            project_m(1, 1)
            project_e(0, 0)
            project_e(1, 1)
            for k in range(3, LATE):
                transpose_x(k, k % 2)
                project(k - 1, (k - 1) % 2)
                if k == 3:
                    pe.wait_ge(sq_done, 1)
                    nc.tensor.transpose(pS[:, 0:P], sl_sq[:], ident[:]).then_inc(slT_made, 1)
            steps(pe, LATE - 1, NT - 1, lambda k, slot, half: project(k, slot))
            project(NT - 1, 1)
            pe.wait_ge(pE_read, NT - 1)
            pe.wait_ge(pM_read, NT - 1)
            neighbour_sums(0, 0)
            attention_sums(0, 0)
            beside_copies(1, 1, 0)
            steps(pe, 2, NT - 1, beside_copies)
            neighbour_sums(NT - 1, 1)
            pe.wait_ge(others_summed, 1)
            pe.wait_ge(sl_bc_done, 1)
            nc.tensor.matmul(pS[0:1, 0:1], others_sum[:], ones[:, 0:1], start=True, stop=True).then_inc(others_added, 1)
            pe.wait_ge(eT_done, NT - 1)
            for cols, bank, done in ((slice(RIGHT.start, EW), pE[1], right_summed), (LEFT, pE[0], att_done)):
                pe.wait_ge(mix_done, NT - 2 if bank is pE[1] else NT - 1)
                for k in range(NT):
                    last = nc.tensor.matmul(bank[:, cols], eT[:, 1, k, :], hD[:, k, cols], start=k == 0, stop=k == NT - 1)
                last.then_inc(done, 1)

            def general_sums(past):
                def one_tile(t, slot, _):
                    pe.wait_ge(adjT_done, t + past)
                    pe.wait_ge(eT_done, t + past)
                    pe.wait_ge(xb_gated_done, t + (past - 1))
                    pe.wait_ge(mix_done, t + (past - 1))
                    for k in range(NT):
                        nc.tensor.matmul(pM[slot][:, 0:MW], adjT[:, slot, k, :], xw_hi[:, k, :].bitcast(fp32),
                                         start=k == 0, stop=False)
                        last = nc.tensor.matmul(pM[slot][:, 0:MW], adjT[:, slot, k, :], xw_lo[:, k, :].bitcast(fp32),
                                                start=False, stop=k == NT - 1)
                    last.then_inc(nbr_done, 1)
                    for k in range(NT):
                        last = nc.tensor.matmul(pE[slot][:, 0:EW], eT[:, slot, k, :], hD[:, k, 0:EW],
                                                start=k == 0, stop=k == NT - 1)
                    last.then_inc(att_done, 1)

                steps(pe, 0, NT, one_tile)

            second_pass(pe, general_sums)


_INS = ['x', 'adj', 'L0_gnn_W_sa', 'L0_gnn_a_sa', 'L0_gnn_W_gcnb', 'L0_gnn_b_gcnb', 'L0_gnn_Wa', 'L0_gnn_ba',
        'L0_gnn_Wb', 'L0_gnn_bb']
_OUT_SHAPE, _OUT_DTYPE = (2048, 256), 'float32'


def kernel(**inputs):
    import numpy as _np
    import concourse.bacc as _bacc
    from concourse import mybir as _mybir
    from concourse.bass_utils import run_bass_kernel_spmd as _run

    nc = _bacc.Bacc("TRN2", target_bir_lowering=False, num_devices=1)
    arrays, args = {}, []
    for name in _INS:
        a = _np.ascontiguousarray(inputs[name])
        arrays[f"in_{name}_dram"] = a
        args.append(nc.dram_tensor(f"in_{name}_dram", a.shape, _mybir.dt.from_np(a.dtype), kind="ExternalInput").ap())
    args.append(nc.dram_tensor("out_dram", _OUT_SHAPE, _mybir.dt.from_np(_np.dtype(_OUT_DTYPE)),
                               kind="ExternalOutput").ap())
    gated_two_relation_gnn_kernel(nc, *args)
    r = _run(nc, [arrays], core_ids=[0])
    return r.results[0]["out_dram"]
```
